# Optimizing a Trainium2 kernel written in Bass

```python
import numpy as np
import jax
import jax.numpy as jnp

def _softmax(x, axis=-1):
    return jax.nn.softmax(x, axis=axis)

def _gelu(x):
    return jax.nn.gelu(x, approximate=True)

def _silu(x):
    return jax.nn.silu(x)

def _sigmoid(x):
    return jax.nn.sigmoid(x)

def _layernorm(x, axis=-1, eps=1e-05):
    m = jnp.mean(x, axis=axis, keepdims=True)
    v = jnp.var(x, axis=axis, keepdims=True)
    return (x - m) / jnp.sqrt(v + eps)

def _scatter_add(tgt, idx, src, axis=0):
    return tgt.at[idx].add(src)

def _segment_sum(src, seg, n):
    return jax.ops.segment_sum(src, seg, n)
kernel_name = 'mk_adaln_ffn_d2_seqx_r4_25aa64'

def setup_inputs(seed: int=0):
    np.random.seed(seed)
    _w = jnp.asarray

    def _rec_inputs():
        import jax
        import jax.numpy as jnp
        _rk = jax.random.key(seed)
        x = -7.109e-05 + 0.9999 * jax.random.normal(jax.random.fold_in(_rk, 1), (32, 64, 1024), jnp.float32)
        _lenS = 64 - jax.random.randint(jax.random.fold_in(_rk, 7), (32,), 0, max(1, 64 // 4) + 1, jnp.int32)
        _lenS2 = 64 - jax.random.randint(jax.random.fold_in(_rk, 8), (32,), 0, max(1, 64 // 4) + 1, jnp.int32)
        itok_B_0_15 = jax.random.randint(jax.random.fold_in(_rk, 11), (32,), 0, 16, jnp.int32)
        return (x, itok_B_0_15)
    x, itok_B_0_15 = _rec_inputs()

    def _L0_cond_setup():
        import jax, jax.numpy as jnp
        import numpy as np
        MAX_LORAS = 16
        IN, OUT = (1024, 1024)
        B, S = (8, 512)
        key = jax.random.key(seed)
        k1, k2, k3 = jax.random.split(key, 3)
        x = jax.random.normal(k1, (B, S, IN), dtype=jnp.float32)
        adapter_ids = jax.random.randint(k2, (B,), 0, MAX_LORAS)
        weight = jax.random.normal(k3, (MAX_LORAS, OUT, IN), dtype=jnp.float32) * 0.02
        return {'x': x, 'adapter_ids': adapter_ids, 'weight': weight}
    _L0_cond_all = _L0_cond_setup()
    _L0_cond_in = {k: v for k, v in _L0_cond_all.items() if k in ('weight',)}
    del _L0_cond_all

    def _L0_ffn_setup():
        import jax, jax.numpy as jnp
        import numpy as np
        B, S, D, O, E, R = (2, 1024, 1024, 1024, 8, 16)
        TOP_K = 2
        SCALING = 32.0 / 16.0
        key = jax.random.key(seed)
        k = jax.random.split(key, 6)
        x = jax.random.normal(k[0], (B, S, D), dtype=jnp.float32)
        W_base = jax.random.normal(k[1], (O, D), dtype=jnp.float32) * 0.02
        b_base = jax.random.normal(k[2], (O,), dtype=jnp.float32) * 0.02
        W_router = jax.random.normal(k[3], (E, D), dtype=jnp.float32) * 0.01
        lora_A = jax.random.normal(k[4], (E, R, D), dtype=jnp.float32) * (1.0 / np.sqrt(D))
        lora_B = jax.random.normal(k[5], (E, O, R), dtype=jnp.float32) * 0.02
        return {'x': x, 'W_base': W_base, 'b_base': b_base, 'W_router': W_router, 'lora_A': lora_A, 'lora_B': lora_B}
    _L0_ffn_all = _L0_ffn_setup()
    _L0_ffn_in = {k: v for k, v in _L0_ffn_all.items() if k in ('W_base', 'b_base', 'W_router', 'lora_A', 'lora_B')}
    del _L0_ffn_all

    def _L1_cond_setup():
        import jax, jax.numpy as jnp
        import numpy as np
        B, C, T = (64, 64, 1024)
        S, D = (16, 64)
        key = jax.random.key(seed)
        k1, k2, k3 = jax.random.split(key, 3)
        x = jax.random.normal(k1, (B, C, T), dtype=jnp.float32)
        condition = jax.random.randint(k2, (B,), 0, S, dtype=jnp.int64)
        bound = float(np.sqrt(6.0 / C))
        weights = jax.random.uniform(k3, (S, C, D), dtype=jnp.float32, minval=-bound, maxval=bound)
        return {'x': x, 'condition': condition, 'weights': weights}
    _L1_cond_all = _L1_cond_setup()
    _L1_cond_in = {k: v for k, v in _L1_cond_all.items() if k in ('weights',)}
    del _L1_cond_all

    def _L1_ffn_setup():
        import jax, jax.numpy as jnp
        import numpy as np
        B, L, H, Dh, M = (4, 512, 16, 64, 256)
        D = H * Dh
        key = jax.random.key(seed)
        kx, ku, kd, kp = jax.random.split(key, 4)
        x = jax.random.normal(kx, (B, L, D), dtype=jnp.float32)
        up = jax.random.normal(ku, (H, Dh, M), dtype=jnp.float32)
        down = jax.random.normal(kd, (H, M, Dh), dtype=jnp.float32)
        perm = jax.random.permutation(kp, D)
        return {'x': x, 'up': up, 'down': down, 'perm': perm}
    _L1_ffn_all = _L1_ffn_setup()
    _L1_ffn_in = {k: v for k, v in _L1_ffn_all.items() if k in ('up', 'down', 'perm')}
    del _L1_ffn_all
    return {'x': x, 'itok_B_0_15': itok_B_0_15, 'L0_cond_weight': _L0_cond_in['weight'], 'L0_ffn_W_base': _L0_ffn_in['W_base'], 'L0_ffn_b_base': _L0_ffn_in['b_base'], 'L0_ffn_W_router': _L0_ffn_in['W_router'], 'L0_ffn_lora_A': _L0_ffn_in['lora_A'], 'L0_ffn_lora_B': _L0_ffn_in['lora_B'], 'L1_cond_weights': _L1_cond_in['weights'], 'L1_ffn_up': _L1_ffn_in['up'], 'L1_ffn_down': _L1_ffn_in['down'], 'L1_ffn_perm': _L1_ffn_in['perm']}

def reference(x, itok_B_0_15, L0_cond_weight, L0_ffn_W_base, L0_ffn_b_base, L0_ffn_W_router, L0_ffn_lora_A, L0_ffn_lora_B, L1_cond_weights, L1_ffn_up, L1_ffn_down, L1_ffn_perm):
    import jax
    import jax.numpy as jnp

    def _L0_cond_ref(x, adapter_ids, weight):
        import jax, jax.numpy as jnp
        import numpy as np
        MAX_LORAS = 16
        IN, OUT = (1024, 1024)
        B, S = (8, 512)
        w = weight[adapter_ids]
        return jnp.einsum('bsi,boi->bso', x, w)

    def _L0_ffn_ref(x, W_base, b_base, W_router, lora_A, lora_B):
        import jax, jax.numpy as jnp
        import numpy as np
        B, S, D, O, E, R = (2, 1024, 1024, 1024, 8, 16)
        TOP_K = 2
        SCALING = 32.0 / 16.0
        d = x.shape[-1]
        n_experts = W_router.shape[0]
        xf = x.reshape(-1, d)
        logits = xf @ W_router.T
        probs = jax.nn.softmax(logits, axis=-1)
        topk_p, topk_i = jax.lax.top_k(probs, TOP_K)
        topk_p = topk_p / jnp.sum(topk_p, axis=-1, keepdims=True)
        w = jnp.sum(jax.nn.one_hot(topk_i, n_experts, dtype=xf.dtype) * topk_p[..., None], axis=1)
        h = jnp.einsum('td,erd->ter', xf, lora_A)
        lora_out = jnp.einsum('ter,eor,te->to', h, lora_B, w) * SCALING
        base = x @ W_base.T + b_base
        return base + lora_out.reshape(x.shape[:-1] + (W_base.shape[0],))

    def _L1_cond_ref(x, condition, weights):
        import jax, jax.numpy as jnp
        import numpy as np
        B, C, T = (64, 64, 1024)
        S, D = (16, 64)
        W = weights[condition]
        return jnp.einsum('bct,bcd->bdt', x, W)

    def _L1_ffn_ref(x, up, down, perm):
        import jax, jax.numpy as jnp
        import numpy as np
        B, L, H, Dh, M = (4, 512, 16, 64, 256)
        D = H * Dh
        b, l, Dm = x.shape
        h, d = (up.shape[0], up.shape[1])
        unperm = jnp.argsort(perm)
        t = x.reshape(b * l, Dm)
        t = t[:, perm]
        t = t.reshape(b * l, h, d)
        t = jnp.einsum('bhd,hdm->bhm', t, up)
        t = jax.nn.gelu(t, approximate=False)
        t = jnp.einsum('bhm,hmd->bhd', t, down)
        t = t.reshape(b * l, h * d)
        t = t[:, unperm]
        out = t.reshape(b, l, Dm)
        return out
    x = x + _L0_ffn_ref(_L0_cond_ref(x, itok_B_0_15, L0_cond_weight), L0_ffn_W_base, L0_ffn_b_base, L0_ffn_W_router, L0_ffn_lora_A, L0_ffn_lora_B)
    x = x + _L1_ffn_ref(_L1_cond_ref(x, itok_B_0_15, L1_cond_weights), L1_ffn_up, L1_ffn_down, L1_ffn_perm)
    return x

_drawn_inputs = setup_inputs


def setup_inputs(seed=0):
    import zlib

    import numpy as np

    out = dict(_drawn_inputs(seed))
    spreads = {}
    factors = {'L0_ffn_b_base': 2.933}
    for name, (base, spread) in spreads.items():
        noise = np.random.default_rng([zlib.crc32(name.encode()), seed]).standard_normal(out[name].shape)
        drawn = base * np.exp(spread * noise) if base else spread * noise
        out[name] = jnp.asarray(drawn.astype(out[name].dtype))
    for name, factor in factors.items():
        out[name] = (out[name] * factor).astype(out[name].dtype)
    return out
```

```python
from contextlib import ExitStack

import concourse.bass as bass
from concourse import mybir

F32 = mybir.dt.float32
F32R = mybir.dt.float32r
I32 = mybir.dt.int32
ALU = mybir.AluOpType
ACT = mybir.ActivationFunctionType
AX_X = mybir.AxisListType.X

P = 128
SEQS, TOK, D = 32, 64, 1024
IDS = 16
EXPERTS, RANK = 8, 16
HEADS, HD, HIDDEN = 16, 64, 256
ER = EXPERTS * RANK
AR = ER + EXPERTS
KT = D // P
PAIRS = SEQS // 2
GP = 4
GROUPS = PAIRS // GP
GT = GP * P
STEPS = KT
RING = 4
XBUF = 4
HALF = D // 2
SIGN_BIG = -3.0e38


def build(nc, xT, ids, adapters, w_base, b_base, lora_a_router, lora_b, mix, up, down, perm, out):
    ctx = ExitStack()
    with ctx:
        def sb(name, shape, dt=F32):
            return ctx.enter_context(nc.sbuf_tensor(name, shape, dt))

        def sem(name):
            return ctx.enter_context(nc.semaphore(name))

        ring = sb("ring", [P, RING, 2, D])
        base_t = sb("base_t", [P, KT, D])
        c_t = sb("c_t", [P, 2, KT, GT])
        c_pair = sb("c_pair", [P, KT, P])
        c_tok = sb("c_tok", [P, D])
        up_hi = sb("up_hi", [P, HEADS, HIDDEN], F32R)
        up_lo = sb("up_lo", [P, HEADS, HIDDEN], F32R)
        down_sb = sb("down_sb", [P, HEADS, 2, HD])
        x_in = sb("x_in", [P, 2, KT, P])
        ar_sb = sb("ar_sb", [P, KT, AR])
        b_t = sb("b_t", [P, D])
        xres = sb("xres", [P, XBUF, GT])
        y_split = sb("y_split", [P, 2, GT], F32R)
        act_sb = sb("act_sb", [P, 4, GT])
        x1_tok = sb("x1_tok", [P, GT])
        mix_sb = sb("mix_sb", [P, GP, P])
        hw_t = sb("hw_t", [P, 2, GT])
        ident = sb("ident", [P, P])
        bias = sb("bias", [P, KT])
        ids_sb = sb("ids_sb", [1, SEQS], I32)
        perm_sb = sb("perm_sb", [P, KT], I32)
        row_in = sb("row_in", [P, KT], I32)
        row_out = sb("row_out", [P, KT], I32)
        rank_sb = sb("rank_sb", [P, EXPERTS])
        h_l = sb("h_l", [P, AR])
        hw = sb("hw", [P, ER])
        m1 = sb("m1", [P, 1])
        m2 = sb("m2", [P, 1])
        best = sb("best", [P, 2])
        gap = sb("gap", [P, 1])
        th = sb("th", [P, 1])
        score = sb("score", [P, EXPERTS])
        first = sb("first", [P, EXPERTS])
        second = sb("second", [P, EXPERTS])
        rest = sb("rest", [P, EXPERTS])
        wt = sb("wt", [P, 2])
        mixw = sb("mixw", [P, EXPERTS])
        up_raw = c_t[:, 1, :, :].rearrange("p k t -> p (k t)").rearrange("p (h m) -> p h m", h=HEADS)
        base_rows = act_sb[:, :, :].rearrange("p a t -> p (a t)").rearrange("p (b i) -> p b i", b=2)
        b_rows = c_tok[:, :].rearrange("p (j e) -> p j e", j=KT)

        def bank(name):
            return ctx.enter_context(nc.psum_tensor(name, [P, GT], F32))
        acc = [bank("acc0"), bank("acc1")]
        c_ps, tr_ps, y_ps = bank("c_ps"), bank("tr_ps"), bank("y_ps")
        u_ps = [bank("u_ps0"), bank("u_ps1")]
        d_ps = bank("d_ps")

        ids_in, perm_in, ar_in, up_in, down_in = (sem(n) for n in ("ids_in", "perm_in", "ar_in", "up_in", "down_in"))
        b_in, bias_in = sem("b_in"), sem("bias_in")
        base_in = [sem(f"base_in{i}") for i in range(2)]
        x_in_in = [sem(f"x_in_in{i}") for i in range(2)]
        slot_in = [sem(f"slot_in{i}") for i in range(RING)]
        xres_in = [sem(f"xres_in{i}") for i in range(XBUF)]
        stored = [sem(f"stored{i}") for i in range(XBUF)]
        mix_in = sem("mix_in")
        waited = sem("waited")
        consts, ident_ok, rows_ok = sem("consts"), sem("ident_ok"), sem("rows_ok")
        row_in_step, row_out_step = sem("row_in_step"), sem("row_out_step")
        setup_tr, setup_ev, up_hi_ok, up_ok = sem("setup_tr"), sem("setup_ev"), sem("up_hi_ok"), sem("up_ok")
        block_done, c_tok_ok, c_tr_done, c_pair_ok, c_t_ok = (
            sem(n) for n in ("block_done", "c_tok_ok", "c_tr_done", "c_pair_ok", "c_t_ok"))
        router_done, gap_ok, tanh_ok, chain, hw_ok, hw_tr_done, hw_t_ok = (
            sem(n) for n in ("router_done", "gap_ok", "tanh_ok", "chain", "hw_ok", "hw_tr_done", "hw_t_ok"))
        c_done, x1_ok, t_done, x1_tok_ok, y_done, y_hi_ok, y_ok = (
            sem(n) for n in ("c_done", "x1_ok", "t_done", "x1_tok_ok", "y_done", "y_hi_ok", "y_ok"))
        u_done, act_ok, d_done, fin_ok = (sem(n) for n in ("u_done", "act_ok", "d_done", "fin_ok"))

        x_rows = xT.rearrange("d (g t) -> (d g) t", t=GT)
        out_rows = out.rearrange("d (g t) -> (d g) t", t=GT)
        bias_rows = b_base.rearrange("(d a) -> d a", a=1)

        block = ctx.enter_context(nc.Block())

        @block.sync
        def _(sp):
            sp.dma_start(ids_sb[:, :], ids.rearrange("(a s) -> a s", a=1)).then_inc(ids_in, 16)
            sp.dma_start(perm_sb[:, :], perm).then_inc(perm_in, 16)
            sp.wait_ge(ids_in, 16)

            def load_pair(q, half):
                tokens = xT[:, bass.ds(q * P, P)].rearrange("(k p) t -> p k t", p=P)
                sp.dma_start(x_in[:, half, :, :], tokens).then_inc(x_in_in[half], 16)
                chosen = [sp.value_load(ids_sb[0:1, bass.ds(2 * q + z, 1)], min_val=0, max_val=IDS - 1)
                          for z in range(2)]
                for k in range(KT):
                    slot = k % RING
                    if not (isinstance(q, int) and q == 0 and k < RING):
                        sp.wait_ge(block_done, q * KT + k - RING + 1)
                    for z in range(2):
                        sp.dma_start(ring[:, slot, z, :],
                                     adapters[bass.ds(chosen[z], 1), k * P:(k + 1) * P, :]
                                     .rearrange("a p o -> p (a o)")).then_inc(slot_in[slot], 16)

            load_pair(0, 0)
            load_pair(1, 1)
            with sp.Fori(1, PAIRS // 2) as t:
                for half in range(2):
                    sp.wait_ge(block_done, (t * 2 + half - 1) * KT)
                    load_pair(t * 2 + half, half)

        @block.gpsimd
        def _(pool):
            pool.memset(ident[:, :], 0.0).then_inc(ident_ok, 1)
            pool.wait_ge(ident_ok, 1)
            pool.affine_select(out=ident[:, :], in_=ident[:, :], compare_op=ALU.not_equal, fill=1.0, base=0,
                               pattern=[[-1, P]], channel_multiplier=1).then_inc(ident_ok, 1)
            pool.iota(rank_sb[:, :], pattern=[[-1, EXPERTS]], base=EXPERTS, channel_multiplier=0,
                      allow_small_or_imprecise_dtypes=True).then_inc(consts, 1)
            pool.memset(mix_sb[:, :, :], 0.0).then_inc(consts, 1)

            def gather(dst, table, rows, signal):
                pool.indirect_dma_start(dst, None, table, bass.IndirectOffsetOnAxis(ap=rows, axis=0)) \
                    .then_inc(signal, 16)

            pool.wait_ge(perm_in, 16)
            for j in range(KT):
                gather(b_rows[:, j, :], lora_b, perm_sb[:, j:j + 1], b_in)
            for j in range(KT):
                gather(bias[:, j:j + 1], bias_rows, perm_sb[:, j:j + 1], bias_in)
            pool.wait_ge(rows_ok, 2)

            def next_row(rows, stepped, j, n):
                pool.tensor_scalar(rows[:, j:j + 1], rows[:, j:j + 1], 1, None, ALU.add).then_inc(stepped, 1)
                pool.wait_ge(stepped, n + 1)
                on_its_own()

            def on_its_own():
                pool.sem_inc(waited, 1)

            def keep_pair(q, parity, place):
                pool.wait_ge(c_pair_ok, q * 2 + 2)
                pool.tensor_copy(c_t[:, bass.ds(parity, 1), :, place * P:(place + 1) * P]
                                 .rearrange("p a k t -> p (a k) t"), c_pair[:, :, :]).then_inc(c_t_ok, 1)

            def store(g, j):
                next_row(row_out, row_out_step, j, g * STEPS + j)
                pool.wait_ge(fin_ok, g * STEPS + j + 1)
                on_its_own()
                pool.indirect_dma_start(out_rows, bass.IndirectOffsetOnAxis(ap=row_out[:, j:j + 1], axis=0),
                                        xres[:, j % XBUF, :], None).then_inc(stored[j % XBUF], 16)

            def refill(g, j):
                b = j % XBUF
                pool.wait_ge(stored[b], (g * (STEPS // XBUF) + j // XBUF + 1) * 16)
                on_its_own()
                nj = (j + XBUF) % STEPS
                next_row(row_in, row_in_step, nj, g * STEPS + j + XBUF)
                gather(xres[:, b, :], x_rows, row_in[:, nj:nj + 1], xres_in[b])

            for j in range(KT):
                if j >= 2:
                    pool.wait_ge(setup_tr, j)
                gather(base_rows[:, j % 2, :], w_base, perm_sb[:, j:j + 1], base_in[j % 2])
                if j >= KT - XBUF:
                    s = j - (KT - XBUF)
                    next_row(row_in, row_in_step, s, s)
                    gather(xres[:, s, :], x_rows, row_in[:, s:s + 1], xres_in[s])
                if j % 2 == 1 and j > 1:
                    keep_pair(j // 2 - 1, 0, j // 2 - 1)
            keep_pair(GP - 1, 0, GP - 1)
            with pool.Fori(0, GROUPS - 1) as g:
                for j in range(STEPS):
                    if j % 2 == 1:
                        keep_pair(g * GP + GP + j // 2, (g + 1) % 2, j // 2)
                    store(g, j)
                    refill(g, j)
            g = GROUPS - 1
            for j in range(STEPS):
                store(g, j)
                if j < STEPS - XBUF:
                    refill(g, j)
            for b in range(XBUF):
                pool.wait_ge(stored[b], GROUPS * (STEPS // XBUF) * 16)

        @block.tensor
        def _(pe):
            def transposes(dst, srcs, signal):
                for i, src in enumerate(srcs):
                    last = pe.transpose(dst[i // 4][:, (i % 4) * P:(i % 4 + 1) * P], src, ident[:, :])
                last.then_inc(signal, 1)

            def adapter_block(q, k):
                slot = k % RING
                use = q * (KT // RING) + k // RING
                pe.wait_ge(slot_in[slot], use * 32 + 32)
                for h in range(2):
                    for z in range(2):
                        last = pe.matmul(acc[h][z * TOK:(z + 1) * TOK, :], x_half[:, k, z * TOK:(z + 1) * TOK],
                                         ring[:, slot, z, h * HALF:(h + 1) * HALF],
                                         start=(k == 0), stop=(k == KT - 1), skip_group_check=True)
                last.then_inc(block_done, 1)

            x_half = None

            def adapter_blocks(q, place, ks):
                nonlocal x_half
                x_half = x_in[:, place % 2, :, :]
                for k in ks:
                    if k == 0:
                        uses = (q - place % 2) // 2 if isinstance(q, int) else None
                        pe.wait_ge(x_in_in[place % 2], (uses + 1) * 16 if uses is not None
                                   else x_uses(place) * 16)
                        if not (isinstance(q, int) and q == 0):
                            pe.wait_ge(c_pair_ok, q * 2)
                    adapter_block(q, k)

            group = [0]

            def x_uses(place):
                return group[0] * (GP // 2) + GP // 2 + place // 2 + 1

            def turn(q):
                pe.wait_ge(c_tok_ok, q * 2 + 2)
                transposes(acc, [c_tok[:, k * P:(k + 1) * P] for k in range(KT)], c_tr_done)

            def router(q, s=None):
                pe.wait_ge(c_pair_ok, q * 2 + 2)
                if s is not None:
                    pe.wait_ge(x1_tok_ok, s)
                for k in range(KT):
                    last = pe.matmul(tr_ps[:, 0:AR], c_pair[:, k, :], ar_sb[:, k, :],
                                     start=(k == 0), stop=(k == KT - 1))
                last.then_inc(router_done, 1)

            def turn_hw(q):
                pe.wait_ge(hw_ok, q + 1)
                pe.transpose(tr_ps[:, 0:P], hw[:, :], ident[:, :]).then_inc(hw_tr_done, 1)

            def base(j, parity, ks):
                for k in ks:
                    pe.matmul(c_ps[:, :], base_t[:, k, j * P:(j + 1) * P], one(c_t[:, bass.ds(parity, 1), k, :]),
                              start=(k == 0), stop=False)

            def one(ap):
                return ap.rearrange("p a t -> p (a t)")

            def lora(g, j):
                if j == 0:
                    pe.wait_ge(hw_t_ok, g * GP + GP)
                pe.matmul(c_ps[:, :], b_t[:, j * P:(j + 1) * P], one(hw_t[:, bass.ds(g % 2, 1), :]),
                          start=False, stop=True).then_inc(c_done, 1)

            def to_tokens(g, j):
                pe.wait_ge(x1_ok, g * STEPS + j + 1)
                if j % 2 == 0 and not (isinstance(g, int) and g == GROUPS - 1 and j > 0):
                    pe.wait_ge(hw_t_ok, g * GP + GP + j // 2)
                elif j > 0:
                    pe.wait_ge(x1_tok_ok, g * STEPS + j)
                transposes([tr_ps], [xres[:, j % XBUF, p * P:(p + 1) * P] for p in range(GP)], t_done)

            def mix_tokens(g, j):
                pe.wait_ge(x1_tok_ok, g * STEPS + j + 1)
                if j == 0:
                    pe.wait_ge(mix_in, (g * 2 * GP + 2 * GP) * 16)
                for p in range(GP):
                    last = pe.matmul(y_ps[:, p * P:(p + 1) * P], x1_tok[:, p * P:(p + 1) * P], mix_sb[:, p, :],
                                     start=True, stop=True)
                last.then_inc(y_done, 1)

            def up_half(g, j, head):
                s = g * STEPS + j
                if head == 0:
                    pe.wait_ge(y_ok, s + 1)
                for m in range(2):
                    if head == 1:
                        pe.wait_ge(act_ok, s * 4 + m + 1)
                    for w in (up_hi, up_lo):
                        last = pe.matmul(u_ps[m][:, :], w[:, 2 * j + head, m * P:(m + 1) * P],
                                         y_split[:, head, :], start=(w is up_hi), stop=(w is up_lo))
                    last.then_inc(u_done, 1)

            def down_heads(g, j):
                pe.wait_ge(act_ok, (g * STEPS + j) * 4 + 4)
                for m in range(2):
                    for head in range(2):
                        last = pe.matmul(d_ps[head * HD:(head + 1) * HD, :], down_sb[:, 2 * j + head, m, :],
                                         act_sb[:, 2 * head + m, :], start=(m == 0), stop=(m == 1),
                                         skip_group_check=True)
                last.then_inc(d_done, 1)

            pe.wait_ge(ident_ok, 2)
            pe.wait_ge(b_in, KT * 16)
            transposes(u_ps, [b_rows[:, j, :] for j in range(KT)], setup_tr)

            def turn_base(j):
                pe.wait_ge(base_in[j % 2], (j // 2 + 1) * 16)
                pe.wait_ge(setup_ev, 2 * j + 2)
                transposes(u_ps, [base_rows[:, j % 2, k * P:(k + 1) * P] for k in range(KT)], setup_tr)

            adapter_blocks(0, 0, range(KT))
            turn_base(0)
            turn_base(1)
            for q in range(1, GP):
                turn(q - 1)
                turn_base(2 * q)
                if q == 1:
                    pe.wait_ge(ar_in, 16)
                else:
                    pe.wait_ge(hw_t_ok, q - 1)
                router(q - 1)
                adapter_blocks(q, q, range(KT))
                turn_hw(q - 1)
                turn_base(2 * q + 1)
            turn(GP - 1)
            pe.wait_ge(hw_t_ok, GP - 1)
            router(GP - 1)
            pe.wait_ge(setup_ev, 2 * KT + 2)
            pe.wait_ge(c_t_ok, GP)
            base(0, 0, range(KT))
            turn_hw(GP - 1)
            pe.wait_ge(up_ok, 1)
            pe.wait_ge(down_in, 16)

            def steps(g, more):
                group[0] = g
                for j in range(STEPS):
                    place = j // 2
                    q = g * GP + GP + place
                    ks = range(0, KT // 2) if j % 2 == 0 else range(KT // 2, KT)
                    if j > 0:
                        up_half(g, j - 1, 0)
                        if j % 2 == 0 and more:
                            turn(q - 1)
                            up_half(g, j - 1, 1)
                            router(q - 1, g * STEPS + j)
                            base(j, g % 2, range(KT))
                            turn_hw(q - 1)
                        else:
                            base(j, g % 2, range(0, KT // 2))
                            up_half(g, j - 1, 1)
                            base(j, g % 2, range(KT // 2, KT))
                        down_heads(g, j - 1)
                    lora(g, j)
                    if more:
                        adapter_blocks(q, place, ks[0:1])
                    to_tokens(g, j)
                    if more:
                        adapter_blocks(q, place, ks[1:2])
                    mix_tokens(g, j)
                    if more:
                        adapter_blocks(q, place, ks[2:4])
                up_half(g, STEPS - 1, 0)
                if more:
                    q = g * GP + 2 * GP - 1
                    turn(q)
                up_half(g, STEPS - 1, 1)
                if more:
                    router(q, g * STEPS + STEPS)
                    pe.wait_ge(c_t_ok, g * GP + 2 * GP)
                    base(0, (g + 1) % 2, range(KT))
                    turn_hw(q)
                down_heads(g, STEPS - 1)

            with pe.Fori(0, GROUPS - 1) as g:
                steps(g, True)
            steps(GROUPS - 1, False)

        @block.scalar
        def _(act):
            act.dma_start(up_raw[0:HD, :, :], up.rearrange("d (h m) -> d h m", h=HEADS)).then_inc(up_in, 16)
            act.dma_start(up_raw[HD:P, :, :], up.rearrange("d (h m) -> d h m", h=HEADS)).then_inc(up_in, 16)
            act.dma_start(ar_sb[:, :, :], lora_a_router.rearrange("(k p) e -> p k e", p=P)).then_inc(ar_in, 16)
            act.dma_start(down_sb[:, :, :, :], down).then_inc(down_in, 16)

            def load_mix(g):
                for p in range(GP):
                    for z in range(2):
                        e = act.value_load(ids_sb[0:1, bass.ds(g * 2 * GP + 2 * p + z, 1)],
                                           min_val=0, max_val=IDS - 1)
                        act.dma_start(mix_sb[z * TOK:(z + 1) * TOK, p, z * TOK:(z + 1) * TOK],
                                      mix[bass.ds(e, 1), :, :].rearrange("a c d -> c (a d)")).then_inc(mix_in, 16)

            act.wait_ge(ids_in, 16)
            act.wait_ge(consts, 2)
            load_mix(0)

            def out_of_acc(q):
                act.wait_ge(block_done, (q + 1) * KT)
                nc.scalar.copy(c_tok[:, 0:HALF], acc[0][:, :]).then_inc(c_tok_ok, 1)

            def turned(q):
                act.wait_ge(c_tr_done, q + 1)
                if not (isinstance(q, int) and q == 0):
                    act.wait_ge(c_t_ok, q)
                nc.scalar.copy(c_pair[:, 0:KT // 2, :], acc[0][:, :].rearrange("p (k t) -> p k t", t=P)) \
                    .then_inc(c_pair_ok, 1)

            def tanh(q):
                act.wait_ge(gap_ok, q + 1)
                nc.scalar.activation(th[:, :], gap[:, :], ACT.Tanh, scale=0.5).then_inc(tanh_ok, 1)

            def gelu(g, j, i):
                act.wait_ge(u_done, (g * STEPS + j) * 4 + i + 1)
                nc.scalar.activation(act_sb[:, i, :], u_ps[i % 2][:, :], ACT.Gelu).then_inc(act_ok, 1)

            def x1_tokens(g, j):
                act.wait_ge(t_done, g * STEPS + j + 1)
                nc.scalar.copy(x1_tok[:, :], tr_ps[:, :]).then_inc(x1_tok_ok, 1)

            def y_leading(g, j):
                act.wait_ge(y_done, g * STEPS + j + 1)
                for head in range(2):
                    nc.scalar.copy(y_split[0:HD, head, :], y_ps[head * HD:(head + 1) * HD, :]).then_inc(y_hi_ok, 1)

            act.wait_ge(up_in, 32)
            nc.scalar.copy(up_hi[:, :, :], up_raw).then_inc(up_hi_ok, 1)
            act.wait_ge(setup_tr, 1)
            nc.scalar.copy(b_t[:, 0:HALF], u_ps[0][:, :]).then_inc(setup_ev, 1)

            def base_half(j):
                act.wait_ge(setup_tr, j + 2)
                nc.scalar.copy(base_t[:, 0:KT // 2, j * P:(j + 1) * P],
                               u_ps[0][:, :].rearrange("p (k o) -> p k o", o=P)).then_inc(setup_ev, 1)

            out_of_acc(0)
            base_half(0)
            base_half(1)
            for q in range(1, GP):
                turned(q - 1)
                base_half(2 * q)
                tanh(q - 1)
                out_of_acc(q)
                base_half(2 * q + 1)
            turned(GP - 1)
            tanh(GP - 1)

            def steps(g, more):
                for j in range(STEPS):
                    q = g * GP + GP + j // 2 - 1
                    if j > 0:
                        if j % 2 == 0 and more:
                            out_of_acc(q)
                        gelu(g, j - 1, 0)
                        gelu(g, j - 1, 1)
                        if j % 2 == 0 and more:
                            turned(q)
                        gelu(g, j - 1, 2)
                        gelu(g, j - 1, 3)
                        if j % 2 == 0 and more:
                            tanh(q)
                    x1_tokens(g, j)
                    y_leading(g, j)
                q = g * GP + 2 * GP - 1
                if more:
                    load_mix(g + 1)
                    out_of_acc(q)
                gelu(g, STEPS - 1, 0)
                gelu(g, STEPS - 1, 1)
                if more:
                    turned(q)
                gelu(g, STEPS - 1, 2)
                gelu(g, STEPS - 1, 3)
                if more:
                    tanh(q)

            with act.Fori(0, GROUPS - 1) as g:
                steps(g, True)
            steps(GROUPS - 1, False)

        @block.vector
        def _(dve):
            LINKS = 13

            dve.wait_ge(perm_in, 16)
            for rows in (row_in, row_out):
                nc.vector.tensor_scalar(rows[:, :], perm_sb[:, :], GROUPS, -1, ALU.mult, ALU.add).then_inc(rows_ok, 1)

            def out_of_acc(q):
                dve.wait_ge(block_done, (q + 1) * KT)
                nc.vector.tensor_copy(c_tok[:, HALF:D], acc[1][:, :]).then_inc(c_tok_ok, 1)

            def turned(q):
                dve.wait_ge(c_tr_done, q + 1)
                if not (isinstance(q, int) and q == 0):
                    dve.wait_ge(c_t_ok, q)
                nc.vector.tensor_copy(c_pair[:, KT // 2:KT, :], acc[1][:, :].rearrange("p (k t) -> p k t", t=P)) \
                    .then_inc(c_pair_ok, 1)

            def route(q):
                n = [0]

                def link(ins):
                    n[0] += 1
                    ins.then_inc(chain, 1)
                    dve.wait_ge(chain, q * LINKS + n[0])

                logits = h_l[:, ER:AR]
                dve.wait_ge(router_done, q + 1)
                link(nc.vector.tensor_copy(h_l[:, :], tr_ps[:, 0:AR]))
                link(nc.vector.reduce_max(m1[:, :], logits, AX_X))
                link(nc.vector.scalar_tensor_tensor(out=score[:, :], in0=logits, scalar=m1[:, 0:1],
                                                    in1=rank_sb[:, :], op0=ALU.is_equal, op1=ALU.mult))
                link(nc.vector.reduce_max(best[:, 0:1], score[:, :], AX_X))
                link(nc.vector.tensor_scalar(first[:, :], score[:, :], best[:, 0:1], None, ALU.is_equal))
                link(nc.vector.scalar_tensor_tensor(out=rest[:, :], in0=first[:, :], scalar=SIGN_BIG,
                                                    in1=logits, op0=ALU.mult, op1=ALU.add))
                link(nc.vector.reduce_max(m2[:, :], rest[:, :], AX_X))
                nc.vector.tensor_tensor(gap[:, :], m1[:, :], m2[:, :], ALU.subtract).then_inc(gap_ok, 1)
                link(nc.vector.scalar_tensor_tensor(out=score[:, :], in0=rest[:, :], scalar=m2[:, 0:1],
                                                    in1=rank_sb[:, :], op0=ALU.is_equal, op1=ALU.mult))
                link(nc.vector.reduce_max(best[:, 1:2], score[:, :], AX_X))
                link(nc.vector.tensor_scalar(second[:, :], score[:, :], best[:, 1:2], None, ALU.is_equal))
                dve.wait_ge(tanh_ok, q + 1)
                nc.vector.tensor_scalar(wt[:, 0:1], th[:, :], 1.0, None, ALU.add)
                link(nc.vector.tensor_scalar(wt[:, 1:2], th[:, :], -1.0, 1.0, ALU.mult, ALU.add))
                link(nc.vector.tensor_scalar(mixw[:, :], first[:, :], wt[:, 0:1], None, ALU.mult))
                link(nc.vector.scalar_tensor_tensor(out=mixw[:, :], in0=second[:, :], scalar=wt[:, 1:2],
                                                    in1=mixw[:, :], op0=ALU.mult, op1=ALU.add))
                nc.vector.tensor_tensor(hw[:, :].rearrange("p (e r) -> p e r", r=RANK),
                                        h_l[:, 0:ER].rearrange("p (e r) -> p e r", r=RANK),
                                        mixw[:, :].rearrange("p (e a) -> p e a", a=1).broadcast_to([P, EXPERTS, RANK]),
                                        ALU.mult).then_inc(hw_ok, 1)
                assert n[0] == LINKS

            def hw_turned(q, parity, place):
                dve.wait_ge(hw_tr_done, q + 1)
                nc.vector.tensor_copy(hw_t[:, bass.ds(parity, 1), place * P:(place + 1) * P]
                                      .rearrange("p a t -> p (a t)"), tr_ps[:, 0:P]).then_inc(hw_t_ok, 1)

            def layer0_out(g, j):
                b = j % XBUF
                dve.wait_ge(c_done, g * STEPS + j + 1)
                dve.wait_ge(xres_in[b], (g * (STEPS // XBUF) + j // XBUF + 1) * 16)
                nc.vector.scalar_tensor_tensor(out=xres[:, b, :], in0=c_ps[:, :], scalar=bias[:, j:j + 1],
                                               in1=xres[:, b, :], op0=ALU.add, op1=ALU.add).then_inc(x1_ok, 1)

            def y_rest(g, j):
                dve.wait_ge(y_hi_ok, (g * STEPS + j) * 2 + 2)
                for head in range(2):
                    last = nc.vector.tensor_tensor(y_split[HD:P, head, :], y_ps[head * HD:(head + 1) * HD, :],
                                                   y_split[0:HD, head, :].bitcast(F32), ALU.subtract)
                last.then_inc(y_ok, 1)

            def result(g, j):
                b = j % XBUF
                dve.wait_ge(d_done, g * STEPS + j + 1)
                nc.vector.tensor_tensor(xres[:, b, :], d_ps[:, :], xres[:, b, :], ALU.add).then_inc(fin_ok, 1)

            dve.wait_ge(up_hi_ok, 1)
            nc.vector.tensor_tensor(up_lo[:, :, :], up_raw, up_hi[:, :, :].bitcast(F32), ALU.subtract).then_inc(up_ok, 1)
            dve.wait_ge(setup_tr, 1)
            nc.vector.tensor_copy(b_t[:, HALF:D], u_ps[1][:, :]).then_inc(setup_ev, 1)

            def base_half(j):
                dve.wait_ge(setup_tr, j + 2)
                nc.vector.tensor_copy(base_t[:, KT // 2:KT, j * P:(j + 1) * P],
                                      u_ps[1][:, :].rearrange("p (k o) -> p k o", o=P)).then_inc(setup_ev, 1)

            dve.wait_ge(consts, 2)
            out_of_acc(0)
            base_half(0)
            base_half(1)
            for q in range(1, GP):
                turned(q - 1)
                base_half(2 * q)
                route(q - 1)
                out_of_acc(q)
                hw_turned(q - 1, 0, q - 1)
                base_half(2 * q + 1)
            turned(GP - 1)
            route(GP - 1)
            hw_turned(GP - 1, 0, GP - 1)
            dve.wait_ge(bias_in, KT * 16)

            def steps(g, more):
                for j in range(STEPS):
                    q = g * GP + GP + j // 2 - 1
                    if j > 0:
                        if j % 2 == 0 and more:
                            out_of_acc(q)
                            turned(q)
                            route(q)
                            hw_turned(q, (g + 1) % 2, j // 2 - 1)
                        result(g, j - 1)
                    layer0_out(g, j)
                    y_rest(g, j)
                if more:
                    q = g * GP + 2 * GP - 1
                    out_of_acc(q)
                    turned(q)
                    route(q)
                    hw_turned(q, (g + 1) % 2, GP - 1)
                result(g, STEPS - 1)

            with dve.Fori(0, GROUPS - 1) as g:
                steps(g, True)
            steps(GROUPS - 1, False)


def kernel(x, itok_B_0_15, L0_cond_weight, L0_ffn_W_base, L0_ffn_b_base, L0_ffn_W_router, L0_ffn_lora_A,
           L0_ffn_lora_B, L1_cond_weights, L1_ffn_up, L1_ffn_down, L1_ffn_perm):
    import numpy as np
    import concourse.bacc as bacc
    from concourse.bass_utils import run_bass_kernel_spmd

    x, L0_cond_weight, lora_a, lora_b, router, up, down = (
        np.asarray(a) for a in (x, L0_cond_weight, L0_ffn_lora_A, L0_ffn_lora_B, L0_ffn_W_router, L1_ffn_up, L1_ffn_down))
    arrays = {
        "xT": x.reshape(SEQS * TOK, D).T,
        "ids": np.asarray(itok_B_0_15),
        "adapters": L0_cond_weight.transpose(0, 2, 1),
        "w_base": np.asarray(L0_ffn_W_base),
        "b_base": np.asarray(L0_ffn_b_base),
        "lora_a_router": np.concatenate([lora_a.reshape(ER, D), router], axis=0).T,
        "lora_b": lora_b.transpose(1, 0, 2).reshape(D, ER),
        "mix": np.asarray(L1_cond_weights),
        "up": up.transpose(1, 0, 2).reshape(HD, HEADS * HIDDEN),
        "down": down.reshape(HEADS, 2, P, HD).transpose(2, 0, 1, 3),
        "perm": np.asarray(L1_ffn_perm).reshape(KT, P).T,
    }
    arrays = {k: np.ascontiguousarray(a) for k, a in arrays.items()}
    nc = bacc.Bacc("TRN2", target_bir_lowering=False, num_devices=1)
    args = [nc.dram_tensor(f"{k}_dram", a.shape, mybir.dt.from_np(a.dtype), kind="ExternalInput").ap()
            for k, a in arrays.items()]
    out = nc.dram_tensor("out_dram", (D, SEQS * TOK), F32, kind="ExternalOutput").ap()
    build(nc, *args, out)
    result = run_bass_kernel_spmd(nc, [{f"{k}_dram": a for k, a in arrays.items()}], core_ids=[0])
    return result.results[0]["out_dram"].T.reshape(SEQS, TOK, D)
```

```python
from contextlib import ExitStack

import concourse.bass as bass
from concourse import mybir

F32 = mybir.dt.float32
F32R = mybir.dt.float32r
I32 = mybir.dt.int32
ALU = mybir.AluOpType
ACT = mybir.ActivationFunctionType
AX_X = mybir.AxisListType.X

P = 128
SEQS, TOK, D = 32, 64, 1024
IDS = 16
EXPERTS, RANK = 8, 16
HEADS, HD, HIDDEN = 16, 64, 256
ER = EXPERTS * RANK
AR = ER + EXPERTS
KT = D // P
PAIRS = SEQS // 2
GSEQ = 8
GP = GSEQ // 2
GROUPS = SEQS // GSEQ
GT = GSEQ * TOK
STEPS = KT
LAST = GROUPS * STEPS
XBUF = 4
HALF = D // 2
BIG = -3.0e38
SEQ_BITS = 5
CS = KT // 2


def build(nc, xT, x_seq, ids, adapters, w_base, b_base, lora_a_router, lora_b, mix, up, down, perm, out):
    ctx = ExitStack()
    with ctx:
        def sem(name):
            return ctx.enter_context(nc.semaphore(name))

        start = (nc.sbuf_base + P - 1) // P * P
        used = [0]

        def region(kib):
            used[0] += int(kib * 1024)
            return start + used[0] - int(kib * 1024)

        def at(offset, name, shape, dt=F32):
            return nc.alloc_sbuf_tensor_at(name, shape, dt, offset=offset)

        weights_at = region(64)
        ring = at(weights_at, "ring", [P, KT, 2, D])
        base_t = at(weights_at, "base_t", [P, KT, 2, KT, P], F32R)
        c_all = at(region(64), "c_all", [P, KT, SEQS * TOK])
        split_at = region(32)
        base_rows = at(split_at, "base_rows", [P, KT, D])
        c_hi = at(split_at, "c_hi", [P, KT, GT], F32R)
        c_lo = at(split_at + 16 * 1024, "c_lo", [P, KT, GT], F32R)
        x_in_at = region(8)
        x_in = at(x_in_at, "x_in", [P, 2, 2, KT, TOK])
        up_raw = at(x_in_at, "up_raw", [P, 2, HIDDEN])
        up_hi = at(x_in_at + 2048, "up_hi", [P, 2, HIDDEN], F32R)
        up_lo = at(x_in_at + 4096, "up_lo", [P, 2, HIDDEN], F32R)
        down_sb = at(x_in_at + 6144, "down_sb", [P, 2, 2, 2, HD])
        c_tok_at = region(8)
        c_tok = at(c_tok_at, "c_tok", [P, D])
        grid = at(c_tok_at, "grid", [1, SEQS, SEQS])
        c_pair = at(c_tok_at + 4096, "c_pair", [P, KT, P])
        b_rows = at(c_tok_at + 4096, "b_rows", [P, KT, ER])
        act_sb = at(c_tok_at, "act_sb", [P, 4, GT])
        ar_at = region(4.25)
        ar_sb = at(ar_at, "ar_sb", [P, KT, AR])
        y_split = at(ar_at, "y_split", [P, 2, GT], F32R)
        hw_t = at(region(8), "hw_t", [P, SEQS * TOK])
        b_t = at(region(4), "b_t", [P, D])
        xres = at(region(8), "xres", [P, XBUF, GT])
        x1_tok = at(region(2), "x1_tok", [P, GT])
        mix_sb = at(region(2), "mix_sb", [P, GP, P])
        ident = at(region(0.5), "ident", [P, P])
        bias = at(region(0.03125), "bias", [P, KT])
        perm_sb = at(region(0.03125), "perm_sb", [P, KT], I32)
        row_in = at(region(0.03125), "row_in", [P, KT], I32)
        row_out = at(region(0.03125), "row_out", [P, KT], I32)
        ids_sb = at(region(0.125), "ids_sb", [1, SEQS], I32)
        order = at(region(0.5), "order", [1, 4, SEQS], I32)
        number = at(region(0.125), "number", [1, SEQS])
        key = at(region(0.125), "key", [1, SEQS])
        rank = at(region(0.125), "rank", [1, SEQS])
        ahead = at(region(0.03125), "ahead", [P, EXPERTS])
        h_l = at(region(0.53125), "h_l", [P, AR])
        hw = at(region(0.5), "hw", [P, ER])
        small = [at(region(0.03125), f"small{i}", [P, EXPERTS]) for i in range(7)]
        score, first, second, rest, mixw = small[:5]
        m1, m2, gap, th, best1, best2, w1, w2 = (
            (small[5] if i < 4 else small[6])[:, 2 * (i % 4):2 * (i % 4) + 1] for i in range(8))
        assert used[0] <= nc.sbuf_usable_end - start

        banks = [ctx.enter_context(nc.psum_tensor(f"bank{i}", [P, GT], F32)) for i in range(8)]
        acc = [banks[0:2], banks[2:4]]
        turn_ps, router_ps, hw_ps = banks[4:6], banks[6], banks[7]
        base_ps = banks[0:2]
        u_ps, c_ps, tr_ps, y_ps, d_ps = banks[0:4], banks[4], banks[5], banks[6], banks[7]

        ids_in, perm_in, ar_in, b_in, bias_in, base_in, mix_in, up_in = (
            sem(n) for n in ("ids_in", "perm_in", "ar_in", "b_in", "bias_in", "base_in", "mix_in", "up_in"))
        x_in_in = [sem(f"x_in_in{i}") for i in range(2)]
        slot_in = [[sem(f"slot_in{z}_{k}") for k in range(KT)] for z in range(2)]
        xres_in = [sem(f"xres_in{i}") for i in range(XBUF)]
        stored = [sem(f"stored{i}") for i in range(XBUF)]
        down_in = [sem(f"down_in{i}") for i in range(2)]
        waited = sem("waited")
        ident_ok, consts, number_ok, sorting, order_ok, rows_ok, row_in_step, row_out_step = (
            sem(n) for n in ("ident_ok", "consts", "number_ok", "sorting", "order_ok", "rows_ok", "row_in_step",
                             "row_out_step"))
        b_tr, b_t_ok, base_tr, base_hi_ok, base_ok = (
            sem(n) for n in ("b_tr", "b_t_ok", "base_tr", "base_hi_ok", "base_ok"))
        block_done, c_tok_ok, turn_done, c_pair_ok, c_kept = (
            sem(n) for n in ("block_done", "c_tok_ok", "turn_done", "c_pair_ok", "c_kept"))
        router_done, gap_ok, tanh_ok, chain, hw_ok, hw_tr_done, hw_t_ok = (
            sem(n) for n in ("router_done", "gap_ok", "tanh_ok", "chain", "hw_ok", "hw_tr_done", "hw_t_ok"))
        c_hi_ok, c_lo_ok, up_hi_ok, up_ok = (sem(n) for n in ("c_hi_ok", "c_lo_ok", "up_hi_ok", "up_ok"))
        c_done, x1_ok, tr_done, x1_tok_ok, y_done, y_hi_ok, y_ok = (
            sem(n) for n in ("c_done", "x1_ok", "tr_done", "x1_tok_ok", "y_done", "y_hi_ok", "y_ok"))
        u_done, act_ok, d_done, fin_ok = (sem(n) for n in ("u_done", "act_ok", "d_done", "fin_ok"))

        x_rows = xT.rearrange("d (g t) -> (d g) t", t=GT)
        out_rows = out.rearrange("d (g t) -> (d g) t", t=GT)
        bias_rows = b_base.rearrange("(d a) -> d a", a=1)

        def over_steps(eng, step):
            step(0, 0)
            step(0, 1)
            with eng.Fori(0, GROUPS - 1) as g:
                for j in range(2, STEPS + 2):
                    step(g + j // STEPS, j % STEPS)
            for j in range(2, STEPS):
                step(GROUPS - 1, j)

        def early(g, j, n):
            return isinstance(g, int) and g * STEPS + j < n

        block = ctx.enter_context(nc.Block())

        @block.sync
        def _(sp):
            sp.dma_start(ids_sb[:, :], ids.rearrange("(a s) -> a s", a=1)).then_inc(ids_in, 16)
            sp.dma_start(perm_sb[:, :], perm).then_inc(perm_in, 16)
            sp.wait_ge(order_ok, 1)

            def of_order(row, t, z, most):
                return sp.value_load(order[0:1, row, bass.ds(t + z * PAIRS, 1)], min_val=0, max_val=most)

            def load_pair(t, half):
                for z in range(2):
                    seq = of_order(2, t, z, SEQS - 1)
                    sp.dma_start(x_in[:, half, z, :, :],
                                 x_seq[bass.ds(seq, 1), :, :, :].rearrange("a p k t -> p (a k) t")) \
                        .then_inc(x_in_in[half], 16)
                which = [of_order(1, t, z, IDS - 1) for z in range(2)]
                changed = None if isinstance(t, int) and t == 0 else [of_order(3, t, z, 1) for z in range(2)]

                def rows(z, k):
                    sp.dma_start(ring[:, k, z, :], adapters[bass.ds(which[z], 1), k * P:(k + 1) * P, :]
                                 .rearrange("a p o -> p (a o)")).then_inc(slot_in[z][k], 16)

                for k in range(KT):
                    for z in range(2):
                        if changed is None:
                            rows(z, k)
                            continue
                        with sp.If(changed[z]):
                            sp.wait_ge(block_done, (t - 1) * KT + k + 1)
                            rows(z, k)
                        with sp.Else():
                            sp.wait_ge(slot_in[z][k], t * 16)
                            sp.sem_inc(slot_in[z][k], 16)

            load_pair(0, 0)
            load_pair(1, 1)
            with sp.Fori(1, PAIRS // 2) as i:
                for half in range(2):
                    sp.wait_ge(block_done, (i * 2 + half - 1) * KT)
                    load_pair(i * 2 + half, half)

            def load_up(j):
                for z in range(2):
                    sp.dma_start(up_raw[z * HD:(z + 1) * HD, :, :],
                                 up[:, 2 * j * HIDDEN:(2 * j + 2) * HIDDEN].rearrange("d (h m) -> d h m", h=2)) \
                        .then_inc(up_in, 16)

            def load_down(j):
                sp.dma_start(down_sb[:, j % 2, :, :, :], down[:, 2 * j:2 * j + 2, :, :]).then_inc(down_in[j % 2], 16)

            def load_mix(g):
                for p in range(GP):
                    for z in range(2):
                        e = sp.value_load(ids_sb[0:1, bass.ds(g * GSEQ + 2 * p + z, 1)], min_val=0, max_val=IDS - 1)
                        sp.dma_start(mix_sb[z * TOK:(z + 1) * TOK, p, z * TOK:(z + 1) * TOK],
                                     mix[bass.ds(e, 1), :, :].rearrange("a c d -> c (a d)")).then_inc(mix_in, 16)

            sp.wait_ge(consts, 2)
            load_mix(0)
            sp.wait_ge(block_done, PAIRS * KT)
            load_up(0)
            load_down(0)
            load_down(1)

            def steps(g, more):
                for j in range(STEPS):
                    if more or j + 1 < STEPS:
                        sp.wait_ge(up_ok, g * STEPS + j + 1)
                        load_up((j + 1) % STEPS)
                    if more and j == STEPS - 1:
                        sp.wait_ge(y_done, g * STEPS + STEPS)
                        load_mix(g + 1)
                    if more or j + 2 < STEPS:
                        sp.wait_ge(d_done, g * STEPS + j + 1)
                        load_down((j + 2) % STEPS)

            with sp.Fori(0, GROUPS - 1) as g:
                steps(g, True)
            steps(GROUPS - 1, False)

        @block.gpsimd
        def _(pool):
            def on_its_own():
                pool.sem_inc(waited, 1)

            def gather(dst, table, rows, signal):
                pool.indirect_dma_start(dst, None, table, bass.IndirectOffsetOnAxis(ap=rows, axis=0)) \
                    .then_inc(signal, 16)

            def next_row(rows, stepped, j, n):
                pool.tensor_scalar(rows[:, j:j + 1], rows[:, j:j + 1], 1, None, ALU.add).then_inc(stepped, 1)
                pool.wait_ge(stepped, n + 1)
                on_its_own()

            pool.iota(number[:, :], pattern=[[1, SEQS]], base=0, channel_multiplier=0,
                      allow_small_or_imprecise_dtypes=True).then_inc(number_ok, 1)
            pool.memset(ident[:, :], 0.0).then_inc(ident_ok, 1)
            pool.wait_ge(ident_ok, 1)
            pool.affine_select(out=ident[:, :], in_=ident[:, :], compare_op=ALU.not_equal, fill=1.0, base=0,
                               pattern=[[-1, P]], channel_multiplier=1).then_inc(ident_ok, 1)
            pool.iota(ahead[:, :], pattern=[[-1, EXPERTS]], base=EXPERTS, channel_multiplier=0,
                      allow_small_or_imprecise_dtypes=True).then_inc(consts, 1)
            pool.memset(mix_sb[:, :, :], 0.0).then_inc(consts, 1)
            pool.sem_inc(c_kept, 2)
            pool.wait_ge(perm_in, 16)
            for j in range(KT):
                gather(b_rows[:, j, :], lora_b, perm_sb[:, j:j + 1], b_in)
            for j in range(KT):
                gather(bias[:, j:j + 1], bias_rows, perm_sb[:, j:j + 1], bias_in)

            def keep_pair(t):
                seqs = [pool.value_load(order[0:1, 2, bass.ds(t + z * PAIRS, 1)], min_val=0, max_val=SEQS - 1)
                        for z in range(2)]
                pool.wait_ge(c_pair_ok, t * 2 + 2)
                on_its_own()
                for z in range(2):
                    pool.tensor_copy(c_all[:, :, bass.ds(seqs[z] * TOK, TOK)], c_pair[:, :, z * TOK:(z + 1) * TOK]) \
                        .then_inc(c_kept, 1)

            pool.wait_ge(order_ok, 1)
            keep_pair(0)
            for j in range(KT):
                gather(base_rows[:, j, :], w_base, perm_sb[:, j:j + 1], base_in)
            pool.wait_ge(rows_ok, 2)
            for s in range(XBUF):
                next_row(row_in, row_in_step, s, s)
                gather(xres[:, s, :], x_rows, row_in[:, s:s + 1], xres_in[s])
            with pool.Fori(1, PAIRS) as t:
                keep_pair(t)

            def store(g, j):
                next_row(row_out, row_out_step, j, g * STEPS + j)
                pool.wait_ge(fin_ok, g * STEPS + j + 1)
                on_its_own()
                pool.indirect_dma_start(out_rows, bass.IndirectOffsetOnAxis(ap=row_out[:, j:j + 1], axis=0),
                                        xres[:, j % XBUF, :], None).then_inc(stored[j % XBUF], 16)

            def refill(g, j):
                b, nj = j % XBUF, (j + XBUF) % STEPS
                next_row(row_in, row_in_step, nj, g * STEPS + j + XBUF)
                pool.wait_ge(stored[b], (g * (STEPS // XBUF) + j // XBUF + 1) * 16)
                on_its_own()
                gather(xres[:, b, :], x_rows, row_in[:, nj:nj + 1], xres_in[b])

            with pool.Fori(0, GROUPS - 1) as g:
                for j in range(STEPS):
                    store(g, j)
                    refill(g, j)
            for j in range(STEPS):
                store(GROUPS - 1, j)
                if j < STEPS - XBUF:
                    refill(GROUPS - 1, j)
            for b in range(XBUF):
                pool.wait_ge(stored[b], GROUPS * (STEPS // XBUF) * 16)

        @block.tensor
        def _(pe):
            def transposes(dst, srcs, signal):
                for i, src in enumerate(srcs):
                    last = pe.transpose(dst[i // 4][:, (i % 4) * P:(i % 4 + 1) * P], src, ident[:, :])
                last.then_inc(signal, 1)

            def adapter_blocks(i, half, ks):
                t = i * 2 + half
                for k in ks:
                    if k == 0:
                        pe.wait_ge(x_in_in[half], i * 32 + 32)
                    for z in range(2):
                        pe.wait_ge(slot_in[z][k], t * 16 + 16)
                    for h in range(2):
                        for z in range(2):
                            last = pe.matmul(acc[half][h][z * TOK:(z + 1) * TOK, :], x_in[:, half, z, k, :],
                                             ring[:, k, z, h * HALF:(h + 1) * HALF],
                                             start=(k == 0), stop=(k == KT - 1), skip_group_check=True)
                    last.then_inc(block_done, 1)

            def turn(t):
                pe.wait_ge(c_tok_ok, t * 2 + 2)
                transposes(turn_ps, [c_tok[:, k * P:(k + 1) * P] for k in range(KT)], turn_done)

            def router(t):
                pe.wait_ge(c_pair_ok, t * 2 + 2)
                for k in range(KT):
                    last = pe.matmul(router_ps[:, 0:AR], c_pair[:, k, :], ar_sb[:, k, :],
                                     start=(k == 0), stop=(k == KT - 1))
                last.then_inc(router_done, 1)

            def turn_hw(t):
                pe.wait_ge(hw_ok, t + 1)
                pe.transpose(hw_ps[:, 0:P], hw[:, :], ident[:, :]).then_inc(hw_tr_done, 1)

            def turn_base(j):
                if j == 0:
                    pe.wait_ge(base_in, KT * 16)
                else:
                    pe.wait_ge(base_ok, j)
                transposes(base_ps, [base_rows[:, j, k * P:(k + 1) * P] for k in range(KT)], base_tr)

            def pair(i, half):
                t = i * 2 + half
                adapter_blocks(i, half, range(0, 2))
                turn(t - 1)
                adapter_blocks(i, half, range(2, 4))
                router(t - 1)
                adapter_blocks(i, half, range(4, 8))
                turn_hw(t - 1)

            pe.wait_ge(ident_ok, 2)
            adapter_blocks(0, 0, range(KT))
            pe.wait_ge(b_in, KT * 16)
            transposes(turn_ps, [b_rows[:, j, :] for j in range(KT)], b_tr)
            pe.wait_ge(ar_in, 16)
            pe.wait_ge(b_t_ok, 2)
            with pe.Fori(0, PAIRS // 2 - 1) as i:
                pair(i, 1)
                pair(i + 1, 0)
            i, t = PAIRS // 2 - 1, PAIRS - 1
            adapter_blocks(i, 1, range(0, 2))
            turn(t - 1)
            turn_base(0)
            adapter_blocks(i, 1, range(2, 4))
            router(t - 1)
            turn_base(1)
            for k in range(4, KT):
                adapter_blocks(i, 1, [k])
                turn_base(k - 2)
            turn_hw(t - 1)
            turn(t)
            turn_base(KT - 2)
            router(t)
            turn_base(KT - 1)
            turn_hw(t)

            def base(g, j, part):
                if part == 0 and not early(g, j, 1):
                    pe.wait_ge(x1_ok, g * STEPS + j)
                if j == 0:
                    pe.wait_ge(c_lo_ok, g * CS + part + 1)
                for k in range(part * KT // CS, (part + 1) * KT // CS):
                    for w, c in ((0, c_hi), (0, c_lo), (1, c_hi)):
                        pe.matmul(c_ps[:, :], base_t[:, j, w, k, :], c[:, k, :],
                                  start=(k == 0 and w == 0 and c is c_hi), stop=False)

            def lora(g, j):
                pe.matmul(c_ps[:, :], b_t[:, j * P:(j + 1) * P], hw_t[:, bass.ds(g * GT, GT)],
                          start=False, stop=True).then_inc(c_done, 1)

            def to_tokens(j):
                transposes([tr_ps], [xres[:, j % XBUF, p * P:(p + 1) * P] for p in range(GP)], tr_done)

            def mix_tokens(g, j):
                pe.wait_ge(x1_tok_ok, g * STEPS + j + 1)
                if j == 0:
                    pe.wait_ge(mix_in, (g + 1) * (GSEQ * 16))
                for p in range(GP):
                    last = pe.matmul(y_ps[:, p * P:(p + 1) * P], x1_tok[:, p * P:(p + 1) * P], mix_sb[:, p, :],
                                     start=True, stop=True)
                last.then_inc(y_done, 1)

            def up_heads(g, j):
                pe.wait_ge(y_ok, g * STEPS + j + 1)
                pe.wait_ge(up_ok, g * STEPS + j + 1)
                for head in range(2):
                    for m in range(2):
                        for w in (up_hi, up_lo):
                            last = pe.matmul(u_ps[2 * head + m][:, :], w[:, head, m * P:(m + 1) * P],
                                             y_split[:, head, :], start=(w is up_hi), stop=(w is up_lo))
                        last.then_inc(u_done, 1)

            def down_heads(g, j):
                pe.wait_ge(act_ok, (g * STEPS + j) * 4 + 4)
                pe.wait_ge(down_in[j % 2], (g * (STEPS // 2) + j // 2 + 1) * 16)
                for m in range(2):
                    for head in range(2):
                        last = pe.matmul(d_ps[head * HD:(head + 1) * HD, :], down_sb[:, j % 2, head, m, :],
                                         act_sb[:, 2 * head + m, :], start=(m == 0), stop=(m == 1),
                                         skip_group_check=True)
                last.then_inc(d_done, 1)

            def step(g, j):
                g1, j1 = (g, j - 1) if j >= 1 else (g - 1, STEPS - 1)
                g2, j2 = (g, j - 2) if j >= 2 else (g - 1, STEPS + j - 2)
                base(g, j, 0)
                if not early(g, j, 1):
                    to_tokens(j1)
                base(g, j, 1)
                if not early(g, j, 2):
                    down_heads(g2, j2)
                if not early(g, j, 1):
                    mix_tokens(g1, j1)
                base(g, j, 2)
                base(g, j, 3)
                lora(g, j)
                if not early(g, j, 1):
                    up_heads(g1, j1)

            pe.wait_ge(base_ok, KT)
            pe.wait_ge(hw_t_ok, PAIRS * 2)
            over_steps(pe, step)
            pe.wait_ge(x1_ok, LAST)
            to_tokens(STEPS - 1)
            down_heads(GROUPS - 1, STEPS - 2)
            mix_tokens(GROUPS - 1, STEPS - 1)
            up_heads(GROUPS - 1, STEPS - 1)
            down_heads(GROUPS - 1, STEPS - 1)

        @block.scalar
        def _(act):
            act.dma_start(ar_sb[:, :, :], lora_a_router.rearrange("(k p) e -> p k e", p=P)).then_inc(ar_in, 16)

            def out_of_acc(t, half):
                act.wait_ge(block_done, (t + 1) * KT)
                nc.scalar.copy(c_tok[:, 0:HALF], acc[half][0][:, :]).then_inc(c_tok_ok, 1)

            def turned(t):
                act.wait_ge(turn_done, t + 1)
                act.wait_ge(c_kept, t * 2 + 2)
                nc.scalar.copy(c_pair[:, 0:KT // 2, :], turn_ps[0][:, :].rearrange("p (k t) -> p k t", t=P)) \
                    .then_inc(c_pair_ok, 1)

            def tanh(t):
                act.wait_ge(gap_ok, t + 1)
                nc.scalar.activation(th, gap, ACT.Tanh, scale=0.5).then_inc(tanh_ok, 1)

            def base_leading(j):
                act.wait_ge(base_tr, j + 1)
                for h in range(2):
                    nc.scalar.copy(base_t[:, j, 0, h * CS:(h + 1) * CS, :],
                                   base_ps[h][:, :].rearrange("p (k o) -> p k o", o=P)).then_inc(base_hi_ok, 1)

            out_of_acc(0, 0)
            act.wait_ge(b_tr, 1)
            nc.scalar.copy(b_t[:, 0:HALF], turn_ps[0][:, :]).then_inc(b_t_ok, 1)
            turned(0)
            tanh(0)

            def pair(t, half):
                out_of_acc(t, half)
                turned(t)
                tanh(t)

            with act.Fori(0, PAIRS // 2 - 2) as i:
                pair(i * 2 + 1, 1)
                pair(i * 2 + 2, 0)
            pair(PAIRS - 3, 1)
            out_of_acc(PAIRS - 2, 0)
            turned(PAIRS - 2)
            base_leading(0)
            tanh(PAIRS - 2)
            for j in range(1, KT - 2):
                base_leading(j)
            out_of_acc(PAIRS - 1, 1)
            turned(PAIRS - 1)
            base_leading(KT - 2)
            tanh(PAIRS - 1)
            base_leading(KT - 1)

            def c_leading(g, part):
                ks = slice(part * KT // CS, (part + 1) * KT // CS)
                nc.scalar.copy(c_hi[:, ks, :], c_all[:, ks, bass.ds(g * GT, GT)]).then_inc(c_hi_ok, 1)

            def gelu(g, j, i):
                act.wait_ge(u_done, (g * STEPS + j) * 4 + i + 1)
                nc.scalar.activation(act_sb[:, i, :], u_ps[i][:, :], ACT.Gelu).then_inc(act_ok, 1)

            def x1_tokens(g, j):
                act.wait_ge(tr_done, g * STEPS + j + 1)
                nc.scalar.copy(x1_tok[:, :], tr_ps[:, :]).then_inc(x1_tok_ok, 1)

            def up_leading(g, j):
                act.wait_ge(up_in, (g * STEPS + j) * 32 + 32)
                nc.scalar.copy(up_hi[:, :, :], up_raw[:, :, :]).then_inc(up_hi_ok, 1)

            def y_leading(g, j):
                act.wait_ge(y_done, g * STEPS + j + 1)
                for head in range(2):
                    nc.scalar.copy(y_split[0:HD, head, :], y_ps[head * HD:(head + 1) * HD, :]).then_inc(y_hi_ok, 1)

            def step(g, j):
                g1, j1 = (g, j - 1) if j >= 1 else (g - 1, STEPS - 1)
                g2, j2 = (g, j - 2) if j >= 2 else (g - 1, STEPS + j - 2)
                if j == 0:
                    if early(g, j, 1):
                        act.wait_ge(c_kept, PAIRS * 2 + 2)
                        act.wait_ge(base_tr, KT)
                    else:
                        act.wait_ge(c_done, g * STEPS)
                    c_leading(g, 0)
                if not early(g, j, 2):
                    gelu(g2, j2, 0)
                    gelu(g2, j2, 1)
                if j == 0:
                    c_leading(g, 1)
                if not early(g, j, 2):
                    gelu(g2, j2, 2)
                    gelu(g2, j2, 3)
                if not early(g, j, 1):
                    x1_tokens(g1, j1)
                if j == 0:
                    c_leading(g, 2)
                    c_leading(g, 3)
                if not early(g, j, 1):
                    up_leading(g1, j1)
                    y_leading(g1, j1)

            over_steps(act, step)
            for i in range(4):
                gelu(GROUPS - 1, STEPS - 2, i)
            x1_tokens(GROUPS - 1, STEPS - 1)
            up_leading(GROUPS - 1, STEPS - 1)
            y_leading(GROUPS - 1, STEPS - 1)
            for i in range(4):
                gelu(GROUPS - 1, STEPS - 1, i)

        @block.vector
        def _(dve):
            LINKS = 13

            n_sort = [0]

            def sorted_by(ins):
                n_sort[0] += 1
                ins.then_inc(sorting, 1)
                dve.wait_ge(sorting, n_sort[0])

            def rows_of(row):
                return row.rearrange("p (a b) -> p a b", a=1).broadcast_to([1, SEQS, SEQS])

            def columns_of(row):
                return row.rearrange("p (a b) -> p a b", b=1).broadcast_to([1, SEQS, SEQS])

            dve.wait_ge(ids_in, 16)
            dve.wait_ge(number_ok, 1)
            sorted_by(nc.vector.tensor_copy(key[:, :], ids_sb[:, :]))
            sorted_by(nc.vector.scalar_tensor_tensor(out=key[:, :], in0=key[:, :], scalar=float(1 << SEQ_BITS),
                                                     in1=number[:, :], op0=ALU.mult, op1=ALU.add))
            sorted_by(nc.vector.tensor_tensor(grid[:, :, :], columns_of(key[:, :]), rows_of(key[:, :]), ALU.is_gt))
            sorted_by(nc.vector.reduce_sum(rank[:, :], grid[:, :, :], AX_X))
            sorted_by(nc.vector.tensor_tensor(grid[:, :, :], columns_of(number[:, :]), rows_of(rank[:, :]),
                                              ALU.is_equal))
            sorted_by(nc.vector.tensor_tensor(grid[:, :, :], grid[:, :, :], rows_of(key[:, :]), ALU.mult))
            sorted_by(nc.vector.reduce_sum(key[:, :], grid[:, :, :], AX_X))
            sorted_by(nc.vector.tensor_copy(order[:, 0, :], key[:, :]))
            sorted_by(nc.vector.tensor_scalar(order[:, 1, :], order[:, 0, :], SEQ_BITS, None, ALU.logical_shift_right))
            sorted_by(nc.vector.tensor_scalar(order[:, 2, :], order[:, 0, :], SEQS - 1, None, ALU.bitwise_and))
            sorted_by(nc.vector.tensor_tensor(order[:, 3, 1:SEQS], order[:, 1, 1:SEQS], order[:, 1, 0:SEQS - 1],
                                              ALU.not_equal))
            for z in range(2):
                last = nc.vector.memset(order[:, 3, z * PAIRS:z * PAIRS + 1], 1)
                if z == 0:
                    sorted_by(last)
            last.then_inc(order_ok, 1)

            dve.wait_ge(perm_in, 16)
            for rows in (row_in, row_out):
                nc.vector.tensor_scalar(rows[:, :], perm_sb[:, :], GROUPS, -1, ALU.mult, ALU.add).then_inc(rows_ok, 1)
            dve.wait_ge(consts, 2)

            def out_of_acc(t, half):
                dve.wait_ge(block_done, (t + 1) * KT)
                nc.vector.tensor_copy(c_tok[:, HALF:D], acc[half][1][:, :]).then_inc(c_tok_ok, 1)

            def turned(t):
                dve.wait_ge(turn_done, t + 1)
                dve.wait_ge(c_kept, t * 2 + 2)
                nc.vector.tensor_copy(c_pair[:, KT // 2:KT, :], turn_ps[1][:, :].rearrange("p (k t) -> p k t", t=P))                     .then_inc(c_pair_ok, 1)

            def route(t):
                n = [0]

                def link(ins):
                    n[0] += 1
                    ins.then_inc(chain, 1)
                    dve.wait_ge(chain, t * LINKS + n[0])

                logits = h_l[:, ER:AR]
                dve.wait_ge(router_done, t + 1)
                link(nc.vector.tensor_copy(h_l[:, :], router_ps[:, 0:AR]))
                link(nc.vector.reduce_max(m1, logits, AX_X))
                link(nc.vector.scalar_tensor_tensor(out=score[:, :], in0=logits, scalar=m1,
                                                    in1=ahead[:, :], op0=ALU.is_equal, op1=ALU.mult))
                link(nc.vector.reduce_max(best1, score[:, :], AX_X))
                link(nc.vector.tensor_scalar(first[:, :], score[:, :], best1, None, ALU.is_equal))
                link(nc.vector.scalar_tensor_tensor(out=rest[:, :], in0=first[:, :], scalar=BIG,
                                                    in1=logits, op0=ALU.mult, op1=ALU.add))
                link(nc.vector.reduce_max(m2, rest[:, :], AX_X))
                nc.vector.tensor_tensor(gap, m1, m2, ALU.subtract).then_inc(gap_ok, 1)
                link(nc.vector.scalar_tensor_tensor(out=score[:, :], in0=rest[:, :], scalar=m2,
                                                    in1=ahead[:, :], op0=ALU.is_equal, op1=ALU.mult))
                link(nc.vector.reduce_max(best2, score[:, :], AX_X))
                link(nc.vector.tensor_scalar(second[:, :], score[:, :], best2, None, ALU.is_equal))
                dve.wait_ge(tanh_ok, t + 1)
                nc.vector.tensor_scalar(w1, th, 1.0, None, ALU.add)
                link(nc.vector.tensor_scalar(w2, th, -1.0, 1.0, ALU.mult, ALU.add))
                link(nc.vector.tensor_scalar(mixw[:, :], first[:, :], w1, None, ALU.mult))
                link(nc.vector.scalar_tensor_tensor(out=mixw[:, :], in0=second[:, :], scalar=w2,
                                                    in1=mixw[:, :], op0=ALU.mult, op1=ALU.add))
                nc.vector.tensor_tensor(hw[:, :].rearrange("p (e r) -> p e r", r=RANK),
                                        h_l[:, 0:ER].rearrange("p (e r) -> p e r", r=RANK),
                                        mixw[:, :].rearrange("p (e a) -> p e a", a=1).broadcast_to([P, EXPERTS, RANK]),
                                        ALU.mult).then_inc(hw_ok, 1)
                assert n[0] == LINKS

            def hw_turned(t):
                seqs = [dve.value_load(order[0:1, 2, bass.ds(t + z * PAIRS, 1)], min_val=0, max_val=SEQS - 1)
                        for z in range(2)]
                dve.wait_ge(hw_tr_done, t + 1)
                for z in range(2):
                    nc.vector.tensor_copy(hw_t[:, bass.ds(seqs[z] * TOK, TOK)], hw_ps[:, z * TOK:(z + 1) * TOK])                         .then_inc(hw_t_ok, 1)

            def base_rest(j):
                dve.wait_ge(base_hi_ok, j * 2 + 2)
                for h in range(2):
                    ks = slice(h * CS, (h + 1) * CS)
                    last = nc.vector.tensor_tensor(base_t[:, j, 1, ks, :],
                                                   base_ps[h][:, :].rearrange("p (k o) -> p k o", o=P),
                                                   base_t[:, j, 0, ks, :].bitcast(F32), ALU.subtract)
                last.then_inc(base_ok, 1)

            def pair(t, half):
                out_of_acc(t, half)
                turned(t)
                route(t)
                hw_turned(t)

            out_of_acc(0, 0)
            dve.wait_ge(b_tr, 1)
            nc.vector.tensor_copy(b_t[:, HALF:D], turn_ps[1][:, :]).then_inc(b_t_ok, 1)
            turned(0)
            route(0)
            hw_turned(0)
            with dve.Fori(0, PAIRS // 2 - 2) as i:
                pair(i * 2 + 1, 1)
                pair(i * 2 + 2, 0)
            pair(PAIRS - 3, 1)
            out_of_acc(PAIRS - 2, 0)
            turned(PAIRS - 2)
            base_rest(0)
            route(PAIRS - 2)
            for j in range(1, KT - 2):
                base_rest(j)
            hw_turned(PAIRS - 2)
            out_of_acc(PAIRS - 1, 1)
            turned(PAIRS - 1)
            base_rest(KT - 2)
            route(PAIRS - 1)
            base_rest(KT - 1)
            hw_turned(PAIRS - 1)
            dve.wait_ge(bias_in, KT * 16)

            def c_rest(g, part):
                ks = slice(part * KT // CS, (part + 1) * KT // CS)
                dve.wait_ge(c_hi_ok, g * CS + part + 1)
                nc.vector.tensor_tensor(c_lo[:, ks, :], c_all[:, ks, bass.ds(g * GT, GT)],
                                        c_hi[:, ks, :].bitcast(F32), ALU.subtract).then_inc(c_lo_ok, 1)

            def layer0_out(g, j):
                b = j % XBUF
                dve.wait_ge(c_done, g * STEPS + j + 1)
                dve.wait_ge(xres_in[b], (g * (STEPS // XBUF) + j // XBUF + 1) * 16)
                nc.vector.scalar_tensor_tensor(out=xres[:, b, :], in0=c_ps[:, :], scalar=bias[:, j:j + 1],
                                               in1=xres[:, b, :], op0=ALU.add, op1=ALU.add).then_inc(x1_ok, 1)

            def up_rest(g, j):
                dve.wait_ge(up_hi_ok, g * STEPS + j + 1)
                nc.vector.tensor_tensor(up_lo[:, :, :], up_raw[:, :, :], up_hi[:, :, :].bitcast(F32),
                                        ALU.subtract).then_inc(up_ok, 1)

            def y_rest(g, j):
                dve.wait_ge(y_hi_ok, (g * STEPS + j) * 2 + 2)
                for head in range(2):
                    last = nc.vector.tensor_tensor(y_split[HD:P, head, :], y_ps[head * HD:(head + 1) * HD, :],
                                                   y_split[0:HD, head, :].bitcast(F32), ALU.subtract)
                last.then_inc(y_ok, 1)

            def result(g, j):
                b = j % XBUF
                dve.wait_ge(d_done, g * STEPS + j + 1)
                nc.vector.tensor_tensor(xres[:, b, :], d_ps[:, :], xres[:, b, :], ALU.add).then_inc(fin_ok, 1)

            def step(g, j):
                g1, j1 = (g, j - 1) if j >= 1 else (g - 1, STEPS - 1)
                g2, j2 = (g, j - 2) if j >= 2 else (g - 1, STEPS + j - 2)
                if j == 0:
                    for part in range(CS):
                        c_rest(g, part)
                if not early(g, j, 2):
                    result(g2, j2)
                if not early(g, j, 1):
                    up_rest(g1, j1)
                    y_rest(g1, j1)
                layer0_out(g, j)

            over_steps(dve, step)
            result(GROUPS - 1, STEPS - 2)
            up_rest(GROUPS - 1, STEPS - 1)
            y_rest(GROUPS - 1, STEPS - 1)
            result(GROUPS - 1, STEPS - 1)


def kernel(x, itok_B_0_15, L0_cond_weight, L0_ffn_W_base, L0_ffn_b_base, L0_ffn_W_router, L0_ffn_lora_A,
           L0_ffn_lora_B, L1_cond_weights, L1_ffn_up, L1_ffn_down, L1_ffn_perm):
    import numpy as np
    import concourse.bacc as bacc
    from concourse.bass_utils import run_bass_kernel_spmd

    x, L0_cond_weight, lora_a, lora_b, router, up, down = (
        np.asarray(a) for a in (x, L0_cond_weight, L0_ffn_lora_A, L0_ffn_lora_B, L0_ffn_W_router, L1_ffn_up, L1_ffn_down))
    arrays = {
        "xT": x.reshape(SEQS * TOK, D).T,
        "x_seq": x.reshape(SEQS, TOK, KT, P).transpose(0, 3, 2, 1),
        "ids": np.asarray(itok_B_0_15),
        "adapters": L0_cond_weight.transpose(0, 2, 1),
        "w_base": np.asarray(L0_ffn_W_base),
        "b_base": np.asarray(L0_ffn_b_base),
        "lora_a_router": np.concatenate([lora_a.reshape(ER, D), router], axis=0).T,
        "lora_b": lora_b.transpose(1, 0, 2).reshape(D, ER),
        "mix": np.asarray(L1_cond_weights),
        "up": up.transpose(1, 0, 2).reshape(HD, HEADS * HIDDEN),
        "down": down.reshape(HEADS, 2, P, HD).transpose(2, 0, 1, 3),
        "perm": np.asarray(L1_ffn_perm).reshape(KT, P).T,
    }
    arrays = {k: np.ascontiguousarray(a) for k, a in arrays.items()}
    nc = bacc.Bacc("TRN2", target_bir_lowering=False, num_devices=1)
    args = [nc.dram_tensor(f"{k}_dram", a.shape, mybir.dt.from_np(a.dtype), kind="ExternalInput").ap()
            for k, a in arrays.items()]
    out = nc.dram_tensor("out_dram", (D, SEQS * TOK), F32, kind="ExternalOutput").ap()
    build(nc, *args, out)
    result = run_bass_kernel_spmd(nc, [{f"{k}_dram": a for k, a in arrays.items()}], core_ids=[0])
    return result.results[0]["out_dram"].T.reshape(SEQS, TOK, D)
```

```python
from contextlib import ExitStack

import concourse.bass as bass
from concourse import mybir

F32 = mybir.dt.float32
F32R = mybir.dt.float32r
I32 = mybir.dt.int32
ALU = mybir.AluOpType
ACT = mybir.ActivationFunctionType
AX_X = mybir.AxisListType.X

P = 128
SEQS, TOK, D = 32, 64, 1024
IDS = 16
EXPERTS, RANK = 8, 16
HEADS, HD, HIDDEN = 16, 64, 256
ER = EXPERTS * RANK
AR = ER + EXPERTS
KT = D // P
PAIRS = SEQS // 2
GSEQ = 8
GP = GSEQ // 2
GROUPS = SEQS // GSEQ
GT = GSEQ * TOK
STEPS = KT
LAST = GROUPS * STEPS
XBUF = 4
HALF = D // 2
BIG = -3.0e38
SEQ_BITS = 5
CS = KT // 2


def build(nc, xT, x_seq, ids, adapters, w_base, b_base, lora_a_router, lora_b, mix, up, down, perm, out):
    ctx = ExitStack()
    with ctx:
        def sem(name):
            return ctx.enter_context(nc.semaphore(name))

        start = (nc.sbuf_base + P - 1) // P * P
        used = [0]

        def region(kib):
            used[0] += int(kib * 1024)
            return start + used[0] - int(kib * 1024)

        def at(offset, name, shape, dt=F32):
            return nc.alloc_sbuf_tensor_at(name, shape, dt, offset=offset)

        weights_at = region(64)
        ring = at(weights_at, "ring", [P, KT, 2, D])
        base_t = at(weights_at, "base_t", [P, KT, 2, KT, P], F32R)
        c_at = region(64)
        c_all = at(c_at, "c_all", [P, KT, SEQS * TOK])
        c_lo = at(c_at, "c_lo", [P, KT, SEQS * TOK], F32R)
        split_at = region(32)
        base_rows = at(split_at, "base_rows", [P, KT, KT, P])
        c_hi = at(split_at, "c_hi", [P, KT, GT], F32R)
        b_hi = at(split_at + 4 * 4096, "b_hi", [P, KT, P], F32R)
        hw_hi = at(split_at + 5 * 4096, "hw_hi", [P, GT], F32R)
        x_in_at = region(8)
        x_in = at(x_in_at, "x_in", [P, 2, 2, KT, TOK])
        up_raw = at(x_in_at, "up_raw", [P, 2, HIDDEN])
        up_hi = at(x_in_at + 2048, "up_hi", [P, 2, HIDDEN], F32R)
        up_lo = at(x_in_at + 4096, "up_lo", [P, 2, HIDDEN], F32R)
        down_sb = at(x_in_at + 6144, "down_sb", [P, 2, 2, 2, HD])
        c_tok_at = region(8)
        c_tok = at(c_tok_at, "c_tok", [P, D])
        my_id = at(c_tok_at, "my_id", [SEQS, 1], I32)
        all_ids = at(c_tok_at + 128, "all_ids", [SEQS, SEQS], I32)
        my_number = at(c_tok_at + 256, "my_number", [SEQS, 1])
        number = at(c_tok_at + 384, "number", [SEQS, SEQS])
        my_key = at(c_tok_at + 512, "my_key", [SEQS, 1])
        all_keys = at(c_tok_at + 640, "all_keys", [SEQS, SEQS])
        smaller = at(c_tok_at + 768, "smaller", [SEQS, SEQS])
        rank = at(c_tok_at + 896, "rank", [SEQS, 1])
        placed = at(c_tok_at + 1024, "placed", [SEQS, SEQS])
        ones = at(c_tok_at + 1152, "ones", [SEQS, P])
        c_pair = at(c_tok_at + 4096, "c_pair", [P, KT, P])
        act_sb = at(c_tok_at, "act_sb", [P, 4, GT])
        ar_at = region(4.25)
        ar_sb = at(ar_at, "ar_sb", [P, KT, AR])
        y_split = at(ar_at, "y_split", [P, 2, GT], F32R)
        hw_at, b_at = region(8), region(4)
        hw_t = at(hw_at, "hw_t", [P, SEQS * TOK])
        hw_lo = at(hw_at, "hw_lo", [P, SEQS * TOK], F32R)
        b_rows = at(b_at, "b_rows", [P, KT, ER])
        b_lo = at(b_at, "b_lo", [P, KT, P], F32R)
        xres = at(region(8), "xres", [P, XBUF, GT])
        x1_tok = at(region(2), "x1_tok", [P, GT])
        mix_at = region(4)
        mix_sb = at(mix_at, "mix_sb", [P, 2, GP, P])
        h_l = at(mix_at + 2048, "h_l", [P, AR])
        hw = at(mix_at + 2048 + 544, "hw", [P, ER])
        small = [at(mix_at + 2048 + 544 + 512 + 32 * i, f"small{i}", [P, EXPERTS]) for i in range(7)]
        ident = at(region(0.5), "ident", [P, P])
        bias = at(region(0.03125), "bias", [P, KT])
        perm_sb = at(region(0.03125), "perm_sb", [P, KT], I32)
        row_in = at(region(0.03125), "row_in", [P, KT], I32)
        row_out = at(region(0.03125), "row_out", [P, KT], I32)
        ids_sb = at(region(0.125), "ids_sb", [1, SEQS], I32)
        order = at(region(0.5), "order", [1, 4, SEQS], I32)
        ahead = at(region(0.03125), "ahead", [P, EXPERTS])
        score, first, second, rest, mixw = small[:5]
        m1, m2, gap, th, best1, best2, w1, w2 = (
            (small[5] if i < 4 else small[6])[:, 2 * (i % 4):2 * (i % 4) + 1] for i in range(8))
        assert used[0] <= nc.sbuf_usable_end - start

        banks = [ctx.enter_context(nc.psum_tensor(f"bank{i}", [P, GT], F32)) for i in range(8)]
        acc = [banks[0:2], banks[2:4]]
        turn_ps, router_ps, hw_ps = banks[4:6], banks[6], banks[7]
        base_ps = [banks[4:6], banks[2:4]]
        b_ps = banks[0:2]
        sorted_ps = banks[7]
        u_ps, c_ps, tr_ps, y_ps, d_ps = banks[0:4], banks[4], banks[5], banks[6], banks[7]

        ids_in, sort_ids_in, perm_in, ar_in, b_in, bias_in, mix_in, up_in = (
            sem(n) for n in ("ids_in", "sort_ids_in", "perm_in", "ar_in", "b_in", "bias_in", "mix_in", "up_in"))
        base_in = [sem(f"base_in{j}") for j in range(KT)]
        x_in_in = [sem(f"x_in_in{i}") for i in range(2)]
        slot_in = [[sem(f"slot_in{z}_{k}") for k in range(KT)] for z in range(2)]
        xres_in = [sem(f"xres_in{i}") for i in range(XBUF)]
        stored = [sem(f"stored{i}") for i in range(XBUF)]
        down_in = [sem(f"down_in{i}") for i in range(2)]
        waited = sem("waited")
        mix_cleared = sem("mix_cleared")
        ident_ok, consts, number_ok, sorting, placed_ok, sorted_done, order_ok = (
            sem(n) for n in ("ident_ok", "consts", "number_ok", "sorting", "placed_ok", "sorted_done", "order_ok"))
        rows_ok, row_in_step, row_out_step = (sem(n) for n in ("rows_ok", "row_in_step", "row_out_step"))
        b_tr, b_hi_ok, b_ok, base_tr, base_turned, base_hi_ok, base_ok = (
            sem(n) for n in ("b_tr", "b_hi_ok", "b_ok", "base_tr", "base_turned", "base_hi_ok", "base_ok"))
        block_done, c_tok_ok, turn_done, c_pair_ok, c_kept, last_kept = (
            sem(n) for n in ("block_done", "c_tok_ok", "turn_done", "c_pair_ok", "c_kept", "last_kept"))
        router_done, gap_ok, tanh_ok, chain, hw_ok, hw_tr_done, hw_t_ok = (
            sem(n) for n in ("router_done", "gap_ok", "tanh_ok", "chain", "hw_ok", "hw_tr_done", "hw_t_ok"))
        part_used, c_hi_ok, c_lo_ok, hw_hi_ok, hw_lo_ok, up_hi_ok, up_ok = (
            sem(n) for n in ("part_used", "c_hi_ok", "c_lo_ok", "hw_hi_ok", "hw_lo_ok", "up_hi_ok", "up_ok"))
        c_done, x1_ok, tr_done, x1_tok_ok, y_done, y_hi_ok, y_ok = (
            sem(n) for n in ("c_done", "x1_ok", "tr_done", "x1_tok_ok", "y_done", "y_hi_ok", "y_ok"))
        u_done, act_ok, d_done, fin_ok = (sem(n) for n in ("u_done", "act_ok", "d_done", "fin_ok"))

        x_rows = xT.rearrange("d (g t) -> (d g) t", t=GT)
        out_rows = out.rearrange("d (g t) -> (d g) t", t=GT)
        bias_rows = b_base.rearrange("(d a) -> d a", a=1)

        def over_steps(eng, step):
            step(0, 0)
            step(0, 1)
            with eng.Fori(0, GROUPS - 1) as g:
                for j in range(2, STEPS + 2):
                    step(g + j // STEPS, j % STEPS)
            for j in range(2, STEPS):
                step(GROUPS - 1, j)

        def last_seqs(eng):
            return [eng.value_load(order[0:1, 2, (z + 1) * PAIRS - 1:(z + 1) * PAIRS], min_val=0, max_val=SEQS - 1)
                    for z in range(2)]

        def c_bank(g, j):
            return u_ps[3] if early(g, j, 2) and j == 1 else c_ps

        def early(g, j, n):
            return isinstance(g, int) and g * STEPS + j < n

        block = ctx.enter_context(nc.Block())

        @block.sync
        def _(sp):
            sp.dma_start(perm_sb[:, :], perm).then_inc(perm_in, 16)
            sp.dma_start(my_id[:, :], ids.rearrange("(s a) -> s a", a=1)).then_inc(sort_ids_in, 16)
            sp.dma_start(ids_sb[:, :], ids.rearrange("(a s) -> a s", a=1)).then_inc(ids_in, 16)
            sp.wait_ge(order_ok, 1)

            def of_order(row, t, z, most):
                return sp.value_load(order[0:1, row, bass.ds(t + z * PAIRS, 1)], min_val=0, max_val=most)

            def load_pair(t, half):
                for z in range(2):
                    seq = of_order(2, t, z, SEQS - 1)
                    sp.dma_start(x_in[:, half, z, :, :],
                                 x_seq[bass.ds(seq, 1), :, :, :].rearrange("a p k t -> p (a k) t")) \
                        .then_inc(x_in_in[half], 16)
                which = [of_order(1, t, z, IDS - 1) for z in range(2)]
                changed = None if isinstance(t, int) and t == 0 else [of_order(3, t, z, 1) for z in range(2)]

                def rows(z, k):
                    sp.dma_start(ring[:, k, z, :], adapters[bass.ds(which[z], 1), k * P:(k + 1) * P, :]
                                 .rearrange("a p o -> p (a o)")).then_inc(slot_in[z][k], 16)

                for k in range(KT):
                    for z in range(2):
                        if changed is None:
                            rows(z, k)
                            continue
                        with sp.If(changed[z]):
                            sp.wait_ge(block_done, (t - 1) * KT + k + 1)
                            rows(z, k)
                        with sp.Else():
                            sp.wait_ge(slot_in[z][k], t * 16)
                            sp.sem_inc(slot_in[z][k], 16)

            load_pair(0, 0)
            load_pair(1, 1)
            with sp.Fori(1, PAIRS // 2) as i:
                for half in range(2):
                    sp.wait_ge(block_done, (i * 2 + half - 1) * KT)
                    load_pair(i * 2 + half, half)

            def load_up(j):
                for z in range(2):
                    sp.dma_start(up_raw[z * HD:(z + 1) * HD, :, :],
                                 up[:, 2 * j * HIDDEN:(2 * j + 2) * HIDDEN].rearrange("d (h m) -> d h m", h=2)) \
                        .then_inc(up_in, 16)

            def load_down(j):
                sp.dma_start(down_sb[:, j % 2, :, :, :], down[:, 2 * j:2 * j + 2, :, :]).then_inc(down_in[j % 2], 16)

            def load_mix(g, p):
                which = [sp.value_load(ids_sb[0:1, bass.ds(g * GSEQ + 2 * p + z, 1)], min_val=0, max_val=IDS - 1)
                         for z in range(2)]
                for z in range(2):
                    sp.dma_start(mix_sb[z * TOK:(z + 1) * TOK, bass.ds(g % 2, 1), p, z * TOK:(z + 1) * TOK],
                                 mix[bass.ds(which[z], 1), :, :].rearrange("a c d -> c a d")).then_inc(mix_in, 16)

            sp.wait_ge(ids_in, 16)
            sp.wait_ge(consts, 2)
            for p in range(GP):
                load_mix(0, p)
            sp.wait_ge(block_done, PAIRS * KT)
            load_up(0)
            load_down(0)
            load_down(1)
            sp.wait_ge(mix_cleared, 1)

            def steps(g, more):
                for j in range(STEPS):
                    if more or j + 1 < STEPS:
                        sp.wait_ge(up_ok, g * STEPS + j + 1)
                        load_up((j + 1) % STEPS)
                    if more and 2 <= j < 2 + GP:
                        if j == 2:
                            sp.wait_ge(y_done, g * STEPS + 1)
                        load_mix(g + 1, j - 2)
                    if more or j + 2 < STEPS:
                        sp.wait_ge(d_done, g * STEPS + j + 1)
                        load_down((j + 2) % STEPS)

            with sp.Fori(0, GROUPS - 1) as g:
                steps(g, True)
            steps(GROUPS - 1, False)

        @block.gpsimd
        def _(pool):
            def on_its_own():
                pool.sem_inc(waited, 1)

            def gather(dst, table, rows, signal):
                pool.indirect_dma_start(dst, None, table, bass.IndirectOffsetOnAxis(ap=rows, axis=0)) \
                    .then_inc(signal, 16)

            def next_row(rows, stepped, j, n):
                pool.tensor_scalar(rows[:, j:j + 1], rows[:, j:j + 1], 1, None, ALU.add).then_inc(stepped, 1)
                pool.wait_ge(stepped, n + 1)
                on_its_own()

            pool.iota(number[:, :], pattern=[[1, SEQS]], base=0, channel_multiplier=0,
                      allow_small_or_imprecise_dtypes=True).then_inc(number_ok, 1)
            pool.iota(my_number[:, :], pattern=[[0, 1]], base=0, channel_multiplier=1,
                      allow_small_or_imprecise_dtypes=True).then_inc(number_ok, 1)
            pool.memset(ones[:, :], 1.0).then_inc(number_ok, 1)
            pool.memset(ident[:, :], 0.0).then_inc(ident_ok, 1)
            pool.wait_ge(ident_ok, 1)
            pool.affine_select(out=ident[:, :], in_=ident[:, :], compare_op=ALU.not_equal, fill=1.0, base=0,
                               pattern=[[-1, P]], channel_multiplier=1).then_inc(ident_ok, 1)
            pool.iota(ahead[:, :], pattern=[[-1, EXPERTS]], base=EXPERTS, channel_multiplier=0,
                      allow_small_or_imprecise_dtypes=True).then_inc(consts, 1)
            pool.memset(mix_sb[:, 0, :, :], 0.0).then_inc(consts, 1)
            pool.sem_inc(c_kept, 2)
            pool.wait_ge(perm_in, 16)
            for j in range(KT):
                gather(base_rows[:, j, :, :].rearrange("p k o -> p (k o)"), w_base, perm_sb[:, j:j + 1], base_in[j])

            def keep_pair(t):
                seqs = [pool.value_load(order[0:1, 2, bass.ds(t + z * PAIRS, 1)], min_val=0, max_val=SEQS - 1)
                        for z in range(2)]
                pool.wait_ge(c_pair_ok, t * 2 + 2)
                on_its_own()
                for z in range(2):
                    pool.tensor_copy(c_all[:, :, bass.ds(seqs[z] * TOK, TOK)], c_pair[:, :, z * TOK:(z + 1) * TOK]) \
                        .then_inc(c_kept, 1)

            pool.wait_ge(order_ok, 1)
            keep_pair(0)
            for j in range(KT):
                gather(b_rows[:, j, :], lora_b, perm_sb[:, j:j + 1], b_in)
            for j in range(KT):
                gather(bias[:, j:j + 1], bias_rows, perm_sb[:, j:j + 1], bias_in)
            pool.wait_ge(rows_ok, 2)
            for s in range(XBUF):
                next_row(row_in, row_in_step, s, s)
                gather(xres[:, s, :], x_rows, row_in[:, s:s + 1], xres_in[s])
            with pool.Fori(1, PAIRS - 1) as t:
                keep_pair(t)
            pool.wait_ge(hw_t_ok, PAIRS * 2)
            pool.memset(mix_sb[:, 1, :, :], 0.0).then_inc(mix_cleared, 1)

            def store(g, j):
                next_row(row_out, row_out_step, j, g * STEPS + j)
                pool.wait_ge(fin_ok, g * STEPS + j + 1)
                on_its_own()
                pool.indirect_dma_start(out_rows, bass.IndirectOffsetOnAxis(ap=row_out[:, j:j + 1], axis=0),
                                        xres[:, j % XBUF, :], None).then_inc(stored[j % XBUF], 16)

            def refill(g, j):
                b, nj = j % XBUF, (j + XBUF) % STEPS
                next_row(row_in, row_in_step, nj, g * STEPS + j + XBUF)
                pool.wait_ge(stored[b], (g * (STEPS // XBUF) + j // XBUF + 1) * 16)
                on_its_own()
                gather(xres[:, b, :], x_rows, row_in[:, nj:nj + 1], xres_in[b])

            with pool.Fori(0, GROUPS - 1) as g:
                for j in range(STEPS):
                    store(g, j)
                    refill(g, j)
            for j in range(STEPS):
                store(GROUPS - 1, j)
                if j < STEPS - XBUF:
                    refill(GROUPS - 1, j)
            for b in range(XBUF):
                pool.wait_ge(stored[b], GROUPS * (STEPS // XBUF) * 16)

        @block.tensor
        def _(pe):
            def transposes(dst, srcs, signal):
                for i, src in enumerate(srcs):
                    last = pe.transpose(dst[i // 4][:, (i % 4) * P:(i % 4 + 1) * P], src, ident[:, :])
                last.then_inc(signal, 1)

            def adapter_blocks(i, half, ks):
                t = i * 2 + half
                for k in ks:
                    if k == 0:
                        pe.wait_ge(x_in_in[half], i * 32 + 32)
                    for z in range(2):
                        pe.wait_ge(slot_in[z][k], t * 16 + 16)
                    for h in range(2):
                        for z in range(2):
                            last = pe.matmul(acc[half][h][z * TOK:(z + 1) * TOK, :], x_in[:, half, z, k, :],
                                             ring[:, k, z, h * HALF:(h + 1) * HALF],
                                             start=(k == 0), stop=(k == KT - 1), skip_group_check=True)
                    last.then_inc(block_done, 1)

            def turn(t):
                pe.wait_ge(c_tok_ok, t * 2 + 2)
                transposes(turn_ps, [c_tok[:, k * P:(k + 1) * P] for k in range(KT)], turn_done)

            def router(t):
                pe.wait_ge(c_pair_ok, t * 2 + 2)
                for k in range(KT):
                    last = pe.matmul(router_ps[:, 0:AR], c_pair[:, k, :], ar_sb[:, k, :],
                                     start=(k == 0), stop=(k == KT - 1))
                last.then_inc(router_done, 1)

            def turn_hw(t):
                pe.wait_ge(hw_ok, t + 1)
                pe.transpose(hw_ps[:, 0:P], hw[:, :], ident[:, :]).then_inc(hw_tr_done, 1)

            def turn_base(j):
                pe.wait_ge(base_in[j], 16)
                if j >= 2:
                    pe.wait_ge(base_turned, j - 1)
                transposes(base_ps[j % 2], [base_rows[:, j, k, :] for k in range(KT)], base_tr)

            def pair(i, half):
                t = i * 2 + half
                adapter_blocks(i, half, range(0, 2))
                turn(t - 1)
                adapter_blocks(i, half, range(2, 4))
                router(t - 1)
                adapter_blocks(i, half, range(4, 8))
                turn_hw(t - 1)

            pe.wait_ge(placed_ok, 1)
            pe.matmul(sorted_ps[:, 0:SEQS], ones[:, :], placed[:, :], start=True, stop=True).then_inc(sorted_done, 1)
            pe.wait_ge(ident_ok, 2)
            for j in range(KT // 2):
                turn_base(j)
            for k in range(KT // 2):
                adapter_blocks(0, 0, [k])
                turn_base(KT // 2 + k)
            adapter_blocks(0, 0, range(KT // 2, KT))
            pe.wait_ge(base_turned, KT)
            pe.wait_ge(ar_in, 16)
            with pe.Fori(0, PAIRS // 2 - 1) as i:
                pair(i, 1)
                pair(i + 1, 0)
            adapter_blocks(PAIRS // 2 - 1, 1, range(0, 2))
            turn(PAIRS - 2)
            pe.wait_ge(b_in, KT * 16)
            transposes(b_ps, [b_rows[:, j, :] for j in range(KT)], b_tr)
            adapter_blocks(PAIRS // 2 - 1, 1, range(2, 4))
            router(PAIRS - 2)
            adapter_blocks(PAIRS // 2 - 1, 1, range(4, 8))
            turn_hw(PAIRS - 2)
            turn(PAIRS - 1)
            router(PAIRS - 1)

            def base(g, j, part):
                if part == 0 and not early(g, j, 2):
                    pe.wait_ge(x1_ok, g * STEPS + j)
                ks = range(part * KT // CS, (part + 1) * KT // CS)
                if j == 0:
                    pe.wait_ge(c_hi_ok, g * CS + part + 1)
                for k in ks:
                    for w in range(2):
                        pe.matmul(c_bank(g, j)[:, :], base_t[:, j, w, k, :],
                                  c_hi[:, k, :], start=(k == 0 and w == 0), stop=False)
                if j == 0:
                    pe.wait_ge(c_lo_ok, g * CS + part + 1)
                for k in ks:
                    last = pe.matmul(c_bank(g, j)[:, :], base_t[:, j, 0, k, :], c_lo[:, k, bass.ds(g * GT, GT)],
                                     start=False, stop=False)
                if j == STEPS - 1:
                    last.then_inc(part_used, 1)

            def lora(g, j):
                if j == 0:
                    pe.wait_ge(hw_lo_ok, g + 1)
                pe.matmul(c_bank(g, j)[:, :], b_hi[:, j, :], hw_hi[:, :], start=False, stop=False)
                pe.matmul(c_bank(g, j)[:, :], b_lo[:, j, :], hw_hi[:, :], start=False, stop=False)
                pe.matmul(c_bank(g, j)[:, :], b_hi[:, j, :], hw_lo[:, bass.ds(g * GT, GT)],
                          start=False, stop=True).then_inc(c_done, 1)

            def to_tokens(j):
                transposes([tr_ps], [xres[:, j % XBUF, p * P:(p + 1) * P] for p in range(GP)], tr_done)

            def mix_tokens(g, j):
                pe.wait_ge(x1_tok_ok, g * STEPS + j + 1)
                if j == 0:
                    pe.wait_ge(mix_in, (g + 1) * (GSEQ * 16))
                for p in range(GP):
                    last = pe.matmul(y_ps[:, p * P:(p + 1) * P], x1_tok[:, p * P:(p + 1) * P],
                                     mix_sb[:, bass.ds(g % 2, 1), p, :].rearrange("c a d -> c (a d)"),
                                     start=True, stop=True)
                last.then_inc(y_done, 1)

            def up_heads(g, j):
                pe.wait_ge(up_ok, g * STEPS + j + 1)
                for head in range(2):
                    pe.wait_ge(y_ok, (g * STEPS + j) * 2 + head + 1)
                    for m in range(2):
                        for w in (up_hi, up_lo):
                            last = pe.matmul(u_ps[2 * head + m][:, :], w[:, head, m * P:(m + 1) * P],
                                             y_split[:, head, :], start=(w is up_hi), stop=(w is up_lo))
                        last.then_inc(u_done, 1)

            def down_heads(g, j):
                pe.wait_ge(act_ok, (g * STEPS + j) * 4 + 4)
                pe.wait_ge(down_in[j % 2], (g * (STEPS // 2) + j // 2 + 1) * 16)
                for m in range(2):
                    for head in range(2):
                        last = pe.matmul(d_ps[head * HD:(head + 1) * HD, :], down_sb[:, j % 2, head, m, :],
                                         act_sb[:, 2 * head + m, :], start=(m == 0), stop=(m == 1),
                                         skip_group_check=True)
                last.then_inc(d_done, 1)

            def first_step():
                for part in range(CS):
                    base(0, 0, part)
                base(0, 1, 0)
                base(0, 1, 1)
                turn_hw(PAIRS - 1)
                base(0, 1, 2)
                pe.wait_ge(b_ok, 1)
                lora(0, 0)

            def second_step():
                pe.wait_ge(x1_ok, 1)
                to_tokens(0)
                base(0, 1, 3)
                lora(0, 1)
                mix_tokens(0, 0)
                pe.wait_ge(x1_ok, 2)
                up_heads(0, 0)
                pe.wait_ge(base_ok, KT)

            def step(g, j):
                if early(g, j, 1):
                    first_step()
                    return
                if early(g, j, 2):
                    second_step()
                    return
                g1, j1 = (g, j - 1) if j >= 1 else (g - 1, STEPS - 1)
                g2, j2 = (g, j - 2) if j >= 2 else (g - 1, STEPS + j - 2)
                base(g, j, 0)
                to_tokens(j1)
                base(g, j, 1)
                down_heads(g2, j2)
                mix_tokens(g1, j1)
                base(g, j, 2)
                base(g, j, 3)
                lora(g, j)
                up_heads(g1, j1)

            pe.wait_ge(base_ok, 6)
            over_steps(pe, step)
            pe.wait_ge(x1_ok, LAST)
            to_tokens(STEPS - 1)
            mix_tokens(GROUPS - 1, STEPS - 1)
            down_heads(GROUPS - 1, STEPS - 2)
            up_heads(GROUPS - 1, STEPS - 1)
            pe.wait_ge(fin_ok, LAST - 1)
            down_heads(GROUPS - 1, STEPS - 1)

        @block.scalar
        def _(act):
            act.dma_start(all_ids[:, :], ids.rearrange("(a s) -> a s", a=1).broadcast_to([SEQS, SEQS])) \
                .then_inc(sort_ids_in, 16)
            act.dma_start(ar_sb[:, :, :], lora_a_router.rearrange("(k p) e -> p k e", p=P)).then_inc(ar_in, 16)

            def out_of_acc(t, half):
                act.wait_ge(block_done, (t + 1) * KT)
                nc.scalar.copy(c_tok[:, 0:HALF], acc[half][0][:, :]).then_inc(c_tok_ok, 1)

            def turned(t):
                act.wait_ge(turn_done, t + 1)
                act.wait_ge(c_kept, t * 2 + 2)
                nc.scalar.copy(c_pair[:, 0:KT // 2, :], turn_ps[0][:, :].rearrange("p (k t) -> p k t", t=P)) \
                    .then_inc(c_pair_ok, 1)

            def keep_last(half, seqs):
                for z in range(2):
                    nc.scalar.copy(c_all[:, half * KT // 2:(half + 1) * KT // 2, bass.ds(seqs[z] * TOK, TOK)],
                                   turn_ps[half][:, :].rearrange("p (k z t) -> p k z t", z=2, t=TOK)[:, :, z, :]) \
                        .then_inc(last_kept, 1)

            def tanh(t):
                act.wait_ge(gap_ok, t + 1)
                nc.scalar.activation(th, gap, ACT.Tanh, scale=0.5).then_inc(tanh_ok, 1)

            def base_leading(j):
                act.wait_ge(block_done, (PAIRS - 1) * KT + j + 1)
                nc.scalar.copy(base_t[:, j, 0, :, :], base_rows[:, j, :, :]).then_inc(base_hi_ok, 1)

            def pair(t, half):
                out_of_acc(t, half)
                turned(t)
                tanh(t)

            for j in range(KT):
                act.wait_ge(base_tr, j + 1)
                for h in range(2):
                    last = nc.scalar.copy(base_rows[:, j, h * KT // 2:(h + 1) * KT // 2, :],
                                          base_ps[j % 2][h][:, :].rearrange("p (k o) -> p k o", o=P))
                last.then_inc(base_turned, 1)
            pair(0, 0)
            with act.Fori(0, PAIRS // 2 - 2) as i:
                pair(i * 2 + 1, 1)
                pair(i * 2 + 2, 0)
            pair(PAIRS - 3, 1)
            out_of_acc(PAIRS - 2, 0)
            turned(PAIRS - 2)
            for j in range(0, 4):
                base_leading(j)
            tanh(PAIRS - 2)
            for j in range(4, 6):
                base_leading(j)
            act.wait_ge(b_tr, 1)
            act.wait_ge(base_ok, 5)
            for h in range(2):
                last = nc.scalar.copy(b_hi[:, h * KT // 2:(h + 1) * KT // 2, :],
                                      b_ps[h][:, :].rearrange("p (j o) -> p j o", o=P))
            last.then_inc(b_hi_ok, 1)
            seqs = last_seqs(act)
            out_of_acc(PAIRS - 1, 1)
            turned(PAIRS - 1)
            keep_last(0, seqs)

            def c_leading(g, part):
                ks = slice(part * KT // CS, (part + 1) * KT // CS)
                if not (isinstance(g, int) and g == 0):
                    act.wait_ge(part_used, (g - 1) * CS + part + 1)
                nc.scalar.copy(c_hi[:, ks, :], c_all[:, ks, bass.ds(g * GT, GT)]).then_inc(c_hi_ok, 1)

            def hw_leading(g):
                nc.scalar.copy(hw_hi[:, :], hw_t[:, bass.ds(g * GT, GT)]).then_inc(hw_hi_ok, 1)

            def gelu(g, j, i):
                act.wait_ge(u_done, (g * STEPS + j) * 4 + i + 1)
                nc.scalar.activation(act_sb[:, i, :], u_ps[i][:, :], ACT.Gelu).then_inc(act_ok, 1)

            def x1_tokens(g, j):
                act.wait_ge(tr_done, g * STEPS + j + 1)
                nc.scalar.copy(x1_tok[:, :], tr_ps[:, :]).then_inc(x1_tok_ok, 1)

            def up_leading(g, j):
                act.wait_ge(up_in, (g * STEPS + j) * 32 + 32)
                nc.scalar.copy(up_hi[:, :, :], up_raw[:, :, :]).then_inc(up_hi_ok, 1)

            def y_leading(g, j):
                act.wait_ge(y_done, g * STEPS + j + 1)
                for head in range(2):
                    nc.scalar.copy(y_split[0:HD, head, :], y_ps[head * HD:(head + 1) * HD, :]).then_inc(y_hi_ok, 1)

            def step(g, j):
                g1, j1 = (g, j - 1) if j >= 1 else (g - 1, STEPS - 1)
                g2, j2 = (g, j - 2) if j >= 2 else (g - 1, STEPS + j - 2)
                if early(g, j, 1):
                    act.wait_ge(base_ok, 6)
                    act.wait_ge(c_kept, PAIRS * 2)
                    act.wait_ge(last_kept, 4)
                    for part in range(CS):
                        c_leading(g, part)
                    tanh(PAIRS - 1)
                    act.wait_ge(hw_t_ok, PAIRS * 2)
                    hw_leading(g)
                    base_leading(6)
                    base_leading(7)
                elif j == 0:
                    act.wait_ge(c_done, g * STEPS)
                    hw_leading(g)
                splits = j == STEPS - 1 and not (isinstance(g, int) and g == GROUPS - 1)
                if not early(g, j, 2):
                    for i in range(4):
                        gelu(g2, j2, i)
                if splits:
                    c_leading(g + 1, 0)
                if not early(g, j, 1):
                    x1_tokens(g1, j1)
                if splits:
                    c_leading(g + 1, 1)
                if not early(g, j, 1):
                    up_leading(g1, j1)
                    y_leading(g1, j1)
                if splits:
                    c_leading(g + 1, 2)
                    c_leading(g + 1, 3)

            over_steps(act, step)
            for i in range(3):
                gelu(GROUPS - 1, STEPS - 2, i)
            x1_tokens(GROUPS - 1, STEPS - 1)
            gelu(GROUPS - 1, STEPS - 2, 3)
            up_leading(GROUPS - 1, STEPS - 1)
            y_leading(GROUPS - 1, STEPS - 1)
            for i in range(4):
                gelu(GROUPS - 1, STEPS - 1, i)

        @block.vector
        def _(dve):
            LINKS = 13

            n_sort = [0]

            def sorted_by(ins):
                n_sort[0] += 1
                ins.then_inc(sorting, 1)
                dve.wait_ge(sorting, n_sort[0])

            shift = float(1 << SEQ_BITS)
            dve.wait_ge(sort_ids_in, 32)
            dve.wait_ge(number_ok, 3)
            nc.vector.scalar_tensor_tensor(out=my_key[:, :], in0=my_id[:, :], scalar=shift, in1=my_number[:, :],
                                           op0=ALU.mult, op1=ALU.add)
            sorted_by(nc.vector.scalar_tensor_tensor(out=all_keys[:, :], in0=all_ids[:, :], scalar=shift,
                                                     in1=number[:, :], op0=ALU.mult, op1=ALU.add))
            sorted_by(nc.vector.tensor_scalar(smaller[:, :], all_keys[:, :], my_key[:, 0:1], None, ALU.is_lt))
            sorted_by(nc.vector.reduce_sum(rank[:, :], smaller[:, :], AX_X))
            nc.vector.tensor_scalar(placed[:, :], number[:, :], rank[:, 0:1], my_key[:, 0:1], ALU.is_equal, ALU.mult) \
                .then_inc(placed_ok, 1)
            dve.wait_ge(sorted_done, 1)
            sorted_by(nc.vector.tensor_copy(order[:, 0, :], sorted_ps[0:1, 0:SEQS]))
            nc.vector.tensor_scalar(order[:, 2, :], order[:, 0, :], SEQS - 1, None, ALU.bitwise_and)
            sorted_by(nc.vector.tensor_scalar(order[:, 1, :], order[:, 0, :], SEQ_BITS, None, ALU.logical_shift_right))
            sorted_by(nc.vector.tensor_tensor(order[:, 3, 1:SEQS], order[:, 1, 1:SEQS], order[:, 1, 0:SEQS - 1],
                                              ALU.not_equal))
            nc.vector.memset(order[:, 3, 0:1], 1)
            nc.vector.memset(order[:, 3, PAIRS:PAIRS + 1], 1).then_inc(order_ok, 1)

            dve.wait_ge(perm_in, 16)
            for rows in (row_in, row_out):
                nc.vector.tensor_scalar(rows[:, :], perm_sb[:, :], GROUPS, -1, ALU.mult, ALU.add).then_inc(rows_ok, 1)
            dve.wait_ge(consts, 2)

            def out_of_acc(t, half):
                dve.wait_ge(block_done, (t + 1) * KT)
                nc.vector.tensor_copy(c_tok[:, HALF:D], acc[half][1][:, :]).then_inc(c_tok_ok, 1)

            def turned(t):
                dve.wait_ge(turn_done, t + 1)
                dve.wait_ge(c_kept, t * 2 + 2)
                nc.vector.tensor_copy(c_pair[:, KT // 2:KT, :],
                                      turn_ps[1][:, :].rearrange("p (k t) -> p k t", t=P)) \
                    .then_inc(c_pair_ok, 1)

            def route(t):
                n = [0]

                def link(ins):
                    n[0] += 1
                    ins.then_inc(chain, 1)
                    dve.wait_ge(chain, t * LINKS + n[0])

                logits = h_l[:, ER:AR]
                dve.wait_ge(router_done, t + 1)
                link(nc.vector.tensor_copy(h_l[:, :], router_ps[:, 0:AR]))
                link(nc.vector.reduce_max(m1, logits, AX_X))
                link(nc.vector.scalar_tensor_tensor(out=score[:, :], in0=logits, scalar=m1,
                                                    in1=ahead[:, :], op0=ALU.is_equal, op1=ALU.mult))
                link(nc.vector.reduce_max(best1, score[:, :], AX_X))
                link(nc.vector.tensor_scalar(first[:, :], score[:, :], best1, None, ALU.is_equal))
                link(nc.vector.scalar_tensor_tensor(out=rest[:, :], in0=first[:, :], scalar=BIG,
                                                    in1=logits, op0=ALU.mult, op1=ALU.add))
                link(nc.vector.reduce_max(m2, rest[:, :], AX_X))
                nc.vector.tensor_tensor(gap, m1, m2, ALU.subtract).then_inc(gap_ok, 1)
                link(nc.vector.scalar_tensor_tensor(out=score[:, :], in0=rest[:, :], scalar=m2,
                                                    in1=ahead[:, :], op0=ALU.is_equal, op1=ALU.mult))
                link(nc.vector.reduce_max(best2, score[:, :], AX_X))
                link(nc.vector.tensor_scalar(second[:, :], score[:, :], best2, None, ALU.is_equal))
                dve.wait_ge(tanh_ok, t + 1)
                nc.vector.tensor_scalar(w1, th, 1.0, None, ALU.add)
                link(nc.vector.tensor_scalar(w2, th, -1.0, 1.0, ALU.mult, ALU.add))
                link(nc.vector.tensor_scalar(mixw[:, :], first[:, :], w1, None, ALU.mult))
                link(nc.vector.scalar_tensor_tensor(out=mixw[:, :], in0=second[:, :], scalar=w2,
                                                    in1=mixw[:, :], op0=ALU.mult, op1=ALU.add))
                nc.vector.tensor_tensor(hw[:, :].rearrange("p (e r) -> p e r", r=RANK),
                                        h_l[:, 0:ER].rearrange("p (e r) -> p e r", r=RANK),
                                        mixw[:, :].rearrange("p (e a) -> p e a", a=1).broadcast_to([P, EXPERTS, RANK]),
                                        ALU.mult).then_inc(hw_ok, 1)
                assert n[0] == LINKS

            def hw_turned(t):
                seqs = [dve.value_load(order[0:1, 2, bass.ds(t + z * PAIRS, 1)], min_val=0, max_val=SEQS - 1)
                        for z in range(2)]
                dve.wait_ge(hw_tr_done, t + 1)
                for z in range(2):
                    nc.vector.tensor_copy(hw_t[:, bass.ds(seqs[z] * TOK, TOK)], hw_ps[:, z * TOK:(z + 1) * TOK]) \
                        .then_inc(hw_t_ok, 1)

            def keep_last(half, seqs):
                for z in range(2):
                    nc.vector.tensor_copy(c_all[:, half * KT // 2:(half + 1) * KT // 2, bass.ds(seqs[z] * TOK, TOK)],
                                          turn_ps[half][:, :].rearrange("p (k z t) -> p k z t", z=2, t=TOK)
                                          [:, :, z, :]) \
                        .then_inc(last_kept, 1)

            def base_rest(j):
                dve.wait_ge(base_hi_ok, j + 1)
                nc.vector.tensor_tensor(base_t[:, j, 1, :, :], base_rows[:, j, :, :],
                                        base_t[:, j, 0, :, :].bitcast(F32), ALU.subtract).then_inc(base_ok, 1)

            def pair(t, half):
                out_of_acc(t, half)
                turned(t)
                route(t)
                hw_turned(t)

            out_of_acc(0, 0)
            turned(0)
            route(0)
            hw_turned(0)
            with dve.Fori(0, PAIRS // 2 - 2) as i:
                pair(i * 2 + 1, 1)
                pair(i * 2 + 2, 0)
            pair(PAIRS - 3, 1)
            out_of_acc(PAIRS - 2, 0)
            turned(PAIRS - 2)
            for j in range(0, 4):
                base_rest(j)
            route(PAIRS - 2)
            for j in range(4, 6):
                base_rest(j)
            seqs = last_seqs(dve)
            out_of_acc(PAIRS - 1, 1)
            turned(PAIRS - 1)
            keep_last(1, seqs)
            hw_turned(PAIRS - 2)
            dve.wait_ge(b_hi_ok, 1)
            for h in range(2):
                ks = slice(h * KT // 2, (h + 1) * KT // 2)
                last = nc.vector.tensor_tensor(b_lo[:, ks, :], b_ps[h][:, :].rearrange("p (j o) -> p j o", o=P),
                                               b_hi[:, ks, :].bitcast(F32), ALU.subtract)
            last.then_inc(b_ok, 1)
            dve.wait_ge(bias_in, KT * 16)

            def c_rest(g, part):
                ks = slice(part * KT // CS, (part + 1) * KT // CS)
                dve.wait_ge(c_hi_ok, g * CS + part + 1)
                nc.vector.tensor_tensor(c_lo[:, ks, bass.ds(g * GT, GT)], c_all[:, ks, bass.ds(g * GT, GT)],
                                        c_hi[:, ks, :].bitcast(F32), ALU.subtract).then_inc(c_lo_ok, 1)

            def hw_rest(g):
                dve.wait_ge(hw_hi_ok, g + 1)
                nc.vector.tensor_tensor(hw_lo[:, bass.ds(g * GT, GT)], hw_t[:, bass.ds(g * GT, GT)],
                                        hw_hi[:, :].bitcast(F32), ALU.subtract).then_inc(hw_lo_ok, 1)

            def layer0_out(g, j):
                b = j % XBUF
                dve.wait_ge(c_done, g * STEPS + j + 1)
                dve.wait_ge(xres_in[b], (g * (STEPS // XBUF) + j // XBUF + 1) * 16)
                nc.vector.scalar_tensor_tensor(out=xres[:, b, :], in0=c_bank(g, j)[:, :], scalar=bias[:, j:j + 1],
                                               in1=xres[:, b, :], op0=ALU.add, op1=ALU.add).then_inc(x1_ok, 1)

            def up_rest(g, j):
                dve.wait_ge(up_hi_ok, g * STEPS + j + 1)
                nc.vector.tensor_tensor(up_lo[:, :, :], up_raw[:, :, :], up_hi[:, :, :].bitcast(F32),
                                        ALU.subtract).then_inc(up_ok, 1)

            def y_rest(g, j):
                for head in range(2):
                    dve.wait_ge(y_hi_ok, (g * STEPS + j) * 2 + head + 1)
                    nc.vector.tensor_tensor(y_split[HD:P, head, :], y_ps[head * HD:(head + 1) * HD, :],
                                            y_split[0:HD, head, :].bitcast(F32), ALU.subtract).then_inc(y_ok, 1)

            def result(g, j):
                b = j % XBUF
                dve.wait_ge(d_done, g * STEPS + j + 1)
                nc.vector.tensor_tensor(xres[:, b, :], d_ps[:, :], xres[:, b, :], ALU.add).then_inc(fin_ok, 1)

            def step(g, j):
                g1, j1 = (g, j - 1) if j >= 1 else (g - 1, STEPS - 1)
                g2, j2 = (g, j - 2) if j >= 2 else (g - 1, STEPS + j - 2)
                if early(g, j, 1):
                    for part in range(CS):
                        c_rest(g, part)
                    route(PAIRS - 1)
                    hw_turned(PAIRS - 1)
                if j == 0:
                    hw_rest(g)
                splits = j == STEPS - 1 and not (isinstance(g, int) and g == GROUPS - 1)
                if splits:
                    c_rest(g + 1, 0)
                    c_rest(g + 1, 1)
                if not early(g, j, 2):
                    result(g2, j2)
                if not early(g, j, 1):
                    up_rest(g1, j1)
                    y_rest(g1, j1)
                if splits:
                    c_rest(g + 1, 2)
                layer0_out(g, j)
                if splits:
                    c_rest(g + 1, 3)
                if early(g, j, 2) and j == 1:
                    base_rest(6)
                    base_rest(7)

            over_steps(dve, step)
            up_rest(GROUPS - 1, STEPS - 1)
            y_rest(GROUPS - 1, STEPS - 1)
            result(GROUPS - 1, STEPS - 2)
            result(GROUPS - 1, STEPS - 1)


def kernel(x, itok_B_0_15, L0_cond_weight, L0_ffn_W_base, L0_ffn_b_base, L0_ffn_W_router, L0_ffn_lora_A,
           L0_ffn_lora_B, L1_cond_weights, L1_ffn_up, L1_ffn_down, L1_ffn_perm):
    import numpy as np
    import concourse.bacc as bacc
    from concourse.bass_utils import run_bass_kernel_spmd

    x, L0_cond_weight, lora_a, lora_b, router, up, down = (
        np.asarray(a) for a in (x, L0_cond_weight, L0_ffn_lora_A, L0_ffn_lora_B, L0_ffn_W_router, L1_ffn_up, L1_ffn_down))
    arrays = {
        "xT": x.reshape(SEQS * TOK, D).T,
        "x_seq": x.reshape(SEQS, TOK, KT, P).transpose(0, 3, 2, 1),
        "ids": np.asarray(itok_B_0_15),
        "adapters": L0_cond_weight.transpose(0, 2, 1),
        "w_base": np.asarray(L0_ffn_W_base),
        "b_base": np.asarray(L0_ffn_b_base),
        "lora_a_router": np.concatenate([lora_a.reshape(ER, D), router], axis=0).T,
        "lora_b": lora_b.transpose(1, 0, 2).reshape(D, ER),
        "mix": np.asarray(L1_cond_weights),
        "up": up.transpose(1, 0, 2).reshape(HD, HEADS * HIDDEN),
        "down": down.reshape(HEADS, 2, P, HD).transpose(2, 0, 1, 3),
        "perm": np.asarray(L1_ffn_perm).reshape(KT, P).T,
    }
    arrays = {k: np.ascontiguousarray(a) for k, a in arrays.items()}
    nc = bacc.Bacc("TRN2", target_bir_lowering=False, num_devices=1)
    args = [nc.dram_tensor(f"{k}_dram", a.shape, mybir.dt.from_np(a.dtype), kind="ExternalInput").ap()
            for k, a in arrays.items()]
    out = nc.dram_tensor("out_dram", (D, SEQS * TOK), F32, kind="ExternalOutput").ap()
    build(nc, *args, out)
    result = run_bass_kernel_spmd(nc, [{f"{k}_dram": a for k, a in arrays.items()}], core_ids=[0])
    return result.results[0]["out_dram"].T.reshape(SEQS, TOK, D)
```
